# Optimizing a Trainium2 kernel written in Bass

```python
import numpy as np
import jax
import jax.numpy as jnp

def _softmax(x, axis=-1):
    return jax.nn.softmax(x, axis=axis)

def _gelu(x):
    return jax.nn.gelu(x, approximate=True)

def _silu(x):
    return jax.nn.silu(x)

def _sigmoid(x):
    return jax.nn.sigmoid(x)

def _layernorm(x, axis=-1, eps=1e-05):
    m = jnp.mean(x, axis=axis, keepdims=True)
    v = jnp.var(x, axis=axis, keepdims=True)
    return (x - m) / jnp.sqrt(v + eps)

def _scatter_add(tgt, idx, src, axis=0):
    return tgt.at[idx].add(src)

def _segment_sum(src, seg, n):
    return jax.ops.segment_sum(src, seg, n)
kernel_name = 'mk_gnn_resnorm_d2_gnn_r64_429147'

def setup_inputs(seed: int=0):
    np.random.seed(seed)
    _w = jnp.asarray

    def _rec_inputs():
        import jax
        import jax.numpy as jnp
        _gk = jax.random.key(seed)
        x = -0.000202 + 1 * jax.random.normal(jax.random.fold_in(_gk, 1), (100000, 64), jnp.float32)
        src = jax.random.randint(jax.random.fold_in(_gk, 2), (50000,), 0, 100000, jnp.int32)
        dst = jnp.minimum((100000 * jax.random.uniform(jax.random.fold_in(_gk, 3), (50000,)) ** 2.0).astype(jnp.int32), 99999)
        _o = jnp.argsort(dst, stable=True)
        src = src[_o]
        dst = dst[_o]
        edge_attr_32 = -5.16925e-05 + 1.00005 * jax.random.normal(jax.random.fold_in(_gk, 12), (50000, 32), jnp.float32)
        return (x, src, dst, edge_attr_32)
    x, src, dst, edge_attr_32 = _rec_inputs()

    def _L0_gnn_setup():
        import jax, jax.numpy as jnp
        import numpy as np
        N_NODES = 100000
        N_EDGES = 50000
        EDGE_OUT = 32
        HID = 128
        NODE_OUT = 64
        N_GRAPHS = 16
        key = jax.random.key(seed)
        ks = jax.random.split(key, 9)
        x = jax.random.normal(ks[0], (N_NODES, 64), dtype=jnp.float32)
        edge_index = jax.random.randint(ks[1], (2, N_EDGES), 0, N_NODES, dtype=jnp.int64)
        edge_attr = jax.random.normal(ks[2], (N_EDGES, EDGE_OUT), dtype=jnp.float32)
        u = jax.random.normal(ks[3], (N_GRAPHS, 1), dtype=jnp.float32)
        batch = jnp.sort(jax.random.randint(ks[4], (N_NODES,), 0, N_GRAPHS, dtype=jnp.int64))
        d_in = 3 * EDGE_OUT + 1
        W1 = jax.random.normal(ks[5], (d_in, HID), dtype=jnp.float32) / np.sqrt(d_in)
        b1 = jnp.zeros((HID,), dtype=jnp.float32)
        W2 = jax.random.normal(ks[6], (HID, NODE_OUT), dtype=jnp.float32) / np.sqrt(HID)
        b2 = jnp.zeros((NODE_OUT,), dtype=jnp.float32)
        return {'x': x, 'edge_index': edge_index, 'edge_attr': edge_attr, 'u': u, 'batch': batch, 'W1': W1, 'b1': b1, 'W2': W2, 'b2': b2}
    _L0_gnn_all = _L0_gnn_setup()
    _L0_gnn_in = {k: v for k, v in _L0_gnn_all.items() if k in ('u', 'W1', 'b1', 'W2', 'b2')}
    del _L0_gnn_all

    def _L1_gnn_setup():
        import jax, jax.numpy as jnp
        import numpy as np
        N_NODES = 100000
        IN_DIM = 64
        OUT_DIM = 64
        N_EDGES = 25000
        key = jax.random.key(seed)
        k1, k2, k3, k4 = jax.random.split(key, 4)
        x = jax.random.normal(k1, (N_NODES, IN_DIM), dtype=jnp.float32)
        edge_index = jax.random.randint(k2, (2, N_EDGES), 0, N_NODES, dtype=jnp.int32)
        bound = 1.0 / np.sqrt(IN_DIM)
        W = jax.random.uniform(k3, (OUT_DIM, IN_DIM), minval=-bound, maxval=bound, dtype=jnp.float32)
        b = jax.random.uniform(k4, (OUT_DIM,), minval=-bound, maxval=bound, dtype=jnp.float32)
        return {'x': x, 'edge_index': edge_index, 'W': W, 'b': b}
    _L1_gnn_all = _L1_gnn_setup()
    _L1_gnn_in = {k: v for k, v in _L1_gnn_all.items() if k in ('W', 'b')}
    del _L1_gnn_all
    return {'x': x, 'src': src, 'dst': dst, 'edge_attr_32': edge_attr_32, 'L0_gnn_u': _L0_gnn_in['u'], 'L0_gnn_W1': _L0_gnn_in['W1'], 'L0_gnn_b1': _L0_gnn_in['b1'], 'L0_gnn_W2': _L0_gnn_in['W2'], 'L0_gnn_b2': _L0_gnn_in['b2'], 'L1_gnn_W': _L1_gnn_in['W'], 'L1_gnn_b': _L1_gnn_in['b']}

def reference(x, src, dst, edge_attr_32, L0_gnn_u, L0_gnn_W1, L0_gnn_b1, L0_gnn_W2, L0_gnn_b2, L1_gnn_W, L1_gnn_b):
    import jax
    import jax.numpy as jnp

    def _L0_gnn_ref(x, edge_index, edge_attr, u, batch, W1, b1, W2, b2):
        import jax, jax.numpy as jnp
        import numpy as np
        N_NODES = 100000
        N_EDGES = 50000
        EDGE_OUT = 32
        HID = 128
        NODE_OUT = 64
        N_GRAPHS = 16
        N = x.shape[0]
        row = edge_index[0]
        seg_sum = jax.ops.segment_sum(edge_attr, row, num_segments=N)
        seg_max = jax.ops.segment_max(edge_attr, row, num_segments=N)
        cnt = jax.ops.segment_sum(jnp.ones((edge_attr.shape[0], 1), edge_attr.dtype), row, num_segments=N)
        seg_mean = seg_sum / jnp.maximum(cnt, 1.0)
        seg_max = jnp.where(cnt > 0, seg_max, 0.0)
        h = jnp.concatenate([seg_sum, seg_max, seg_mean, u[batch]], axis=1)
        h = jax.nn.relu(h @ W1 + b1)
        return h @ W2 + b2

    def _L1_gnn_ref(x, edge_index, W, b):
        import jax, jax.numpy as jnp
        import numpy as np
        N_NODES = 100000
        IN_DIM = 64
        OUT_DIM = 64
        N_EDGES = 25000
        row, col = (edge_index[0], edge_index[1])
        aggr = jax.ops.segment_sum(x[col], row, num_segments=x.shape[0])
        return jax.nn.relu(aggr @ W.T + b)
    edge_index = jnp.stack([src, dst])
    batch0 = jnp.zeros((100000,), jnp.int32)
    x = _layernorm(x + _L0_gnn_ref(x, edge_index, edge_attr_32, L0_gnn_u, batch0, L0_gnn_W1, L0_gnn_b1, L0_gnn_W2, L0_gnn_b2), axis=-1)
    x = _layernorm(x + _L1_gnn_ref(x, edge_index, L1_gnn_W, L1_gnn_b), axis=-1)
    return x

_drawn_inputs = setup_inputs


def setup_inputs(seed=0):
    import zlib

    import numpy as np

    out = dict(_drawn_inputs(seed))
    spreads = {'L0_gnn_b1': (0.0, 0.1), 'L0_gnn_b2': (0.0, 0.1)}
    factors = {}
    for name, (base, spread) in spreads.items():
        noise = np.random.default_rng([zlib.crc32(name.encode()), seed]).standard_normal(out[name].shape)
        drawn = base * np.exp(spread * noise) if base else spread * noise
        out[name] = jnp.asarray(drawn.astype(out[name].dtype))
    for name, factor in factors.items():
        out[name] = (out[name] * factor).astype(out[name].dtype)
    return out
```

```python
from contextlib import ExitStack

import numpy as np

import concourse.bass as bass
from concourse import mybir

ALU = mybir.AluOpType
ACT = mybir.ActivationFunctionType
AX_X = mybir.AxisListType.X
F32 = mybir.dt.float32
I32 = mybir.dt.int32

P = 128
NODES, FEAT = 100000, 64
EDGES, EFEAT = 50000, 32
HID = 128
EPS = 1e-5
FLT_MAX = float(np.finfo(np.float32).max)

COLS = 512
LEVELS = 16
ROW_LEVELS = 9
EDGE_PARTS = 125
EDGE_COLS = EDGES // EDGE_PARTS
PAIR_COLS = EDGE_COLS // 2
HALF = NODES // 2
CODE0 = 30 * 256
SIGN_CODE = 65536
PAIR_BITS = 15
PAD = 2.0 ** 120
SKIP = 262144.0

TILES = COLS // P
GROUPS = 98
PER = 2
STEPS = GROUPS // PER
CHUNKS = GROUPS * TILES
STEP_CHUNKS = PER * TILES
PAIR_ROW = 2 * (EFEAT + 2)
HALF_ROW = EFEAT + 2

TROWS = 16
TILE = P * TROWS
N_PAD = STEPS * TILE
LAST = NODES - (STEPS - 1) * TILE
LAST_PARTS = LAST // TROWS
LN_ROWS = STEP_CHUNKS + TROWS
assert N_PAD >= NODES and LAST_PARTS * TROWS == LAST and GROUPS * COLS >= EDGES

C0_EARLY = 29


def gnn_kernel(nc, x, src, dst, edge_attr, u, W1, b1, W2, b2, W, b, out):
    edge_pairs = nc.dram_tensor("edge_pairs", (EDGES // 2, PAIR_ROW), F32, kind="Internal").ap()
    node_rows = nc.dram_tensor("node_rows", (N_PAD, 2, FEAT), F32, kind="Internal").ap()
    x1_table = nc.dram_tensor("x1_table", (N_PAD, FEAT), F32, kind="Internal").ap()
    g_table = nc.dram_tensor("g_table", (N_PAD, FEAT), F32, kind="Internal").ap()
    words = nc.dram_tensor("words", (P * COLS + 2,), F32, kind="Internal").ap()
    flags = nc.dram_tensor("flags", (2, P * COLS), F32, kind="Internal").ap()

    node_halves = node_rows.rearrange("n t f -> (n t) f")
    node_pairs = node_rows.rearrange("n t f -> n (t f)")

    with ExitStack() as ctx:
        def sb(name, shape, dt=F32):
            return ctx.enter_context(nc.sbuf_tensor(name, shape, dt))

        def ps(name, shape):
            return ctx.enter_context(nc.psum_tensor(name, shape, F32))

        def sem(name):
            return ctx.enter_context(nc.semaphore(name))

        src_i = sb("src_i", [P, EDGE_COLS], I32)
        dst_i = sb("dst_i", [P, EDGE_COLS], I32)
        src_f = sb("src_f", [P, EDGE_COLS])
        high = sb("high", [P, EDGE_COLS])
        code_i = sb("code_i", [P, EDGE_COLS], I32)
        code_s = sb("code_s", [P, EDGE_COLS], I32)
        pair_i = sb("pair_i", [P, EDGE_COLS], I32)
        pair_tile = sb("pair_tile", [P, PAIR_COLS, 2, HALF_ROW])
        K = [sb(f"K{n}", [P, COLS]) for n in range(2)]
        KT = [sb(f"KT{n}", [P, COLS]) for n in range(2)]
        part_i = sb("part_i", [P, 1], I32)
        bit_a = sb("bit_a", [P, 8], I32)
        bit_b = sb("bit_b", [P, 8], I32)
        sign = sb("sign", [P, 8])
        flip = sb("flip", [P, 8])
        ident = sb("ident", [P, P])
        prev = sb("prev", [P, COLS])
        nxt = sb("nxt", [P, COLS])
        code_here = sb("code_here", [P, COLS], I32)
        code_prev = sb("code_prev", [P, COLS], I32)
        code_next = sb("code_next", [P, COLS], I32)
        pair_bits = sb("pair_bits", [P, COLS], I32)
        same = sb("same", [P, COLS])
        ends = sb("ends", [P, COLS])
        floor_f = sb("floor_f", [P, COLS])
        pair_f = sb("pair_f", [P, COLS])
        twin = sb("twin", [P, COLS])
        upper = sb("upper", [P, COLS])
        node = sb("node", [P, COLS])
        skip = sb("skip", [P, COLS])
        row_f = sb("row_f", [P, COLS])
        sentinel = sb("sentinel", [1, 1])
        pair_idx = sb("pair_idx", [P, GROUPS, TILES], I32)
        row_idx = sb("row_idx", [P, GROUPS, TILES], I32)
        g_idx = sb("g_idx", [P, GROUPS, TILES], I32)
        dst_idx = sb("dst_idx", [P, GROUPS, TILES], I32)
        node_at = sb("node_at", [P, GROUPS, TILES])
        twin_at = sb("twin_at", [P, GROUPS, TILES])
        w1 = sb("w1", [P, HID])
        w1_u = sb("w1_u", [HID, 1])
        b1_c = sb("b1_c", [HID, 1])
        u0 = sb("u0", [P, 1])
        c1 = sb("c1", [HID, 1])
        c1_relu = sb("c1_relu", [HID, P])
        w2 = sb("w2", [HID, FEAT])
        b2_b = sb("b2_b", [P, FEAT])
        w_in = sb("w_in", [FEAT, FEAT])
        w_t = sb("w_t", [FEAT, FEAT])
        b_b = sb("b_b", [P, FEAT])
        eps = sb("eps", [P, 1])
        c0_tile = sb("c0_tile", [P, TROWS, FEAT])
        g0_tile = sb("g0_tile", [P, TROWS, FEAT])
        g0_relu = sb("g0_relu", [P, FEAT])
        g0_sum = sb("g0_sum", [P, 1])
        g0_row = sb("g0_row", [P, FEAT])
        idx_in = [sb(f"idx_in{n}", [P, TILES], I32) for n in range(PER)]
        idx_out = [sb(f"idx_out{n}", [P, TILES], I32) for n in range(PER)]
        pairs = [sb(f"pairs{n}", [P, TILES, PAIR_ROW]) for n in range(PER)]
        wrong = [sb(f"wrong{n}", [P, TILES]) for n in range(PER)]
        odd = [sb(f"odd{n}", [P, TILES], I32) for n in range(PER)]
        same_b = [sb(f"same_b{n}", [FEAT, COLS]) for n in range(PER)]
        floor_b = [sb(f"floor_b{n}", [EFEAT, COLS]) for n in range(PER)]
        feats = [sb(f"feats{n}", [P, COLS]) for n in range(PER)]
        count_r = [sb(f"count_r{n}", [EFEAT, COLS]) for n in range(PER)]
        hidden = [sb(f"hidden{n}", [HID, COLS]) for n in range(PER)]
        delta = [sb(f"delta{n}", [P, TILES, FEAT]) for n in range(PER)]
        near = sb("near", [P, LN_ROWS, 2, FEAT])
        y = sb("y", [P, LN_ROWS, FEAT])
        yc = sb("yc", [P, LN_ROWS, FEAT])
        ysq = sb("ysq", [P, LN_ROWS, FEAT])
        x1 = sb("x1", [P, LN_ROWS, FEAT])
        ysum = sb("ysum", [P, LN_ROWS])
        ymean = sb("ymean", [P, LN_ROWS])
        yvar = sb("yvar", [P, LN_ROWS])
        ystd = sb("ystd", [P, LN_ROWS])
        yrstd = sb("yrstd", [P, LN_ROWS])
        aggr = [sb(f"aggr{n}", [FEAT, COLS]) for n in range(PER)]
        gz = sb("gz", [P, STEP_CHUNKS, FEAT])
        gr = sb("gr", [P, STEP_CHUNKS, FEAT])
        gsum = sb("gsum", [P, STEP_CHUNKS])
        gmean = sb("gmean", [P, STEP_CHUNKS])
        spare = pair_tile[:].rearrange("p q t w -> p (q t w)")

        def carve(k):
            return spare[:, k * TROWS * FEAT:(k + 1) * TROWS * FEAT].rearrange("p (c f) -> p c f", f=FEAT)

        in_x1, in_g, z, zsq, z_out = ([carve(2 * k), carve(2 * k + 1)] for k in range(5))
        zvar = [sb(f"zvar{n}", [P, TROWS]) for n in range(2)]
        zstd = [sb(f"zstd{n}", [P, TROWS]) for n in range(2)]
        zrstd = [sb(f"zrstd{n}", [P, TROWS]) for n in range(2)]

        p_turn = [ps(f"p_turn{n}", [P, COLS]) for n in range(2)]
        p_feat = [ps(f"p_feat{n}", [FEAT, COLS]) for n in range(PER)]
        p_hid = [ps(f"p_hid{n}", [HID, COLS]) for n in range(PER)]
        p_rows_banks = ps("p_rows", [P, PER * COLS])
        p_rows = p_rows_banks[:].rearrange("p (n t f) -> p n t f", n=PER, f=FEAT)[:, :, 0:TILES, :]

        pool_stands, pe_stands, dve_stands = sem("pool_stands"), sem("pe_stands"), sem("dve_stands")
        src_in, dst_in, attr_in = sem("src_in"), sem("dst_in"), sem("attr_in")
        weights_in = sem("weights_in")
        ident_zero, ident_done = sem("ident_zero"), sem("ident_done")
        pair_iota, part_iota = sem("pair_iota"), sem("part_iota")
        ones_done = sem("ones_done")
        setup = sem("setup")
        w_turned, w_t_ready = sem("w_turned"), sem("w_t_ready")
        c1_ready, c1_relu_ready = sem("c1_ready"), sem("c1_relu_ready")
        c0_psum, c0_ready, g0_ready = sem("c0_psum"), sem("c0_ready"), sem("g0_ready")
        g0_relu_done = sem("g0_relu_done")
        pair_ids, pairs_out = sem("pair_ids"), sem("pairs_out")
        sorting = sem("sorting")
        turn_ready, sort_done = sem("turn_ready"), sem("sort_done")
        turned, untangled = sem("turned"), sem("untangled")
        words_out, near_words, flags_out = sem("words_out"), sem("near_words"), sem("flags_out")
        idx_turned, idx_kept = sem("idx_turned"), sem("idx_kept")
        tables = sem("tables")
        c0_out = [sem(f"c0_out{n}") for n in range(2)]
        g0_out, x_out = sem("g0_out"), [sem(f"x_out{n}") for n in range(2)]
        in_idx = [sem(f"in_idx{n}") for n in range(PER)]
        out_idx = [sem(f"out_idx{n}") for n in range(PER)]
        gathered = [sem(f"gathered{n}") for n in range(PER)]
        scattered = [sem(f"scattered{n}") for n in range(PER)]
        flags_in = [sem(f"flags_in{n}") for n in range(PER)]
        edge_known, edge_odd, edge_picked = sem("edge_known"), sem("edge_odd"), sem("edge_picked")
        dst_kept = sem("dst_kept")
        attrs_turned = sem("attrs_turned")
        summed, maxed, inverted, averaged = sem("summed"), sem("maxed"), sem("inverted"), sem("averaged")
        hid_psum, hid_ready, delta_psum, delta_ready = sem("hid_psum"), sem("hid_ready"), sem("delta_psum"), sem("delta_ready")
        g_idx_ready = sem("g_idx_ready")
        l1_in_idx = [sem(f"l1_in_idx{n}") for n in range(PER)]
        l1_out_idx = [sem(f"l1_out_idx{n}") for n in range(PER)]
        l1_gathered, l1_scattered = sem("l1_gathered"), sem("l1_scattered")
        l1_flags_in = [sem(f"l1_flags_in{n}") for n in range(PER)]
        tile_in = sem("tile_in")
        y_ready, ysum_ready, ymean_ready, yc_ready = sem("y_ready"), sem("ysum_ready"), sem("ymean_ready"), sem("yc_ready")
        ysq_ready, yvar_ready, ystd_ready, yrstd_ready = sem("ysq_ready"), sem("yvar_ready"), sem("ystd_ready"), sem("yrstd_ready")
        x1_ready, x1_out = sem("x1_ready"), sem("x1_out")
        x1_turned, aggr_ready, g_psum = sem("x1_turned"), sem("aggr_ready"), sem("g_psum")
        gz_ready, gr_ready, gsum_ready, gmean_ready, g_ready = sem("gz_ready"), sem("gr_ready"), sem("gsum_ready"), sem("gmean_ready"), sem("g_ready")
        z_in = [sem(f"z_in{n}") for n in range(2)]
        z_added, z_squared, zvar_ready, zstd_ready, zrstd_ready, z_done = sem("z_added"), sem("z_squared"), sem("zvar_ready"), sem("zstd_ready"), sem("zrstd_ready"), sem("z_done")
        out_done = [sem(f"out_done{n}") for n in range(2)]

        block = ctx.enter_context(nc.Block())

        def group_of(s, n):
            g = s * PER + n
            return bass.ds(g, 1) if not isinstance(g, int) else slice(g, g + 1)

        def tile_rows(t, parts=P):
            r = t * TILE
            return slice(r, r + parts * TROWS) if isinstance(t, int) else bass.ds(r, parts * TROWS)

        @block.sync
        def _(sp):
            sp.dma_start(src_i[0:EDGE_PARTS, :], src.rearrange("(p c) -> p c", p=EDGE_PARTS)).then_inc(src_in, 16)
            sp.dma_start(w1_u[:], W1[3 * EFEAT, :].rearrange("(h a) -> h a", a=1)).then_inc(weights_in, 16)
            sp.dma_start(b1_c[:], b1.rearrange("(h a) -> h a", a=1)).then_inc(weights_in, 16)
            sp.dma_start(u0[:], u[0, :].partition_broadcast(P)).then_inc(weights_in, 16)
            sp.dma_start(w2[:], W2).then_inc(weights_in, 16)
            sp.dma_start(b2_b[:], b2.partition_broadcast(P)).then_inc(weights_in, 16)
            sp.dma_start(b_b[:], b.partition_broadcast(P)).then_inc(weights_in, 16)
            sp.dma_start(w1[0:EFEAT, :], W1[0:EFEAT, :]).then_inc(weights_in, 16)
            sp.dma_start(w1[2 * EFEAT:4 * EFEAT, :], W1[EFEAT:3 * EFEAT, :]).then_inc(weights_in, 16)
            sp.dma_start(w_in[:], W).then_inc(weights_in, 16)
            sp.dma_start(dst_i[0:EDGE_PARTS, :], dst.rearrange("(p c) -> p c", p=EDGE_PARTS)).then_inc(dst_in, 16)
            attr_v = edge_attr.rearrange("(p q t) f -> p q t f", p=EDGE_PARTS, t=2)
            for t in range(2):
                sp.dma_start(pair_tile[0:EDGE_PARTS, :, t, 0:EFEAT], attr_v[:, :, t, :]).then_inc(attr_in, 16)
            sp.wait_ge(attr_in, 32)
            sp.wait_ge(pair_ids, 2)
            sp.dma_start(edge_pairs.rearrange("(p q) w -> p q w", p=EDGE_PARTS),
                         pair_tile[0:EDGE_PARTS].rearrange("p q t w -> p q (t w)")).then_inc(pairs_out, 16)

            def first_delta(t, n):
                sp.dma_start(node_rows[tile_rows(t), 1, :].rearrange("(p c) f -> p c f", p=P),
                             c0_tile[:]).then_inc(c0_out[n], 16)

            sp.wait_ge(c0_ready, 1)
            first_delta(0, 0)
            first_delta(1, 1)
            with sp.Fori(1, C0_EARLY // 2) as i:
                for n in range(2):
                    sp.wait_ge(c0_out[n], i * 16)
                    first_delta(i * 2 + n, n)
            for t in range(C0_EARLY // 2 * 2, STEPS):
                sp.wait_ge(c0_out[t % 2], t // 2 * 16)
                first_delta(t, t % 2)

            def load_flags(s, n, ready):
                at = (s * PER + n) * COLS
                cols = slice(at, at + COLS) if isinstance(at, int) else bass.ds(at, COLS)
                sp.dma_start(same_b[n][:], flags[0, cols].partition_broadcast(FEAT)).then_inc(ready[n], 16)
                return cols

            def load_idx(slot, table, s, n, ready):
                sp.dma_start(slot[n][:], table[:, group_of(s, n), :].rearrange("p a t -> p (a t)")).then_inc(ready[n], 16)

            def l0_step(s, first=False):
                if not isinstance(s, int) or s < STEPS:
                    for n in range(PER):
                        if not first:
                            sp.wait_ge(gathered[n], s * 16 * TILES)
                        load_idx(idx_in, pair_idx, s, n, in_idx)
                if not first:
                    for n in range(PER):
                        if not (isinstance(s, int) and s == 1):
                            sp.wait_ge(scattered[n], (s - 1) * 16 * TILES)
                        load_idx(idx_out, row_idx, s - 1, n, out_idx)
                if not isinstance(s, int) or s < STEPS:
                    for n in range(PER):
                        if not first:
                            sp.wait_ge(summed, (s - 1) * PER + n + 1)
                            sp.wait_ge(maxed, (s - 1) * PER + n + 1)
                        cols = load_flags(s, n, flags_in)
                        sp.dma_start(floor_b[n][:], flags[1, cols].partition_broadcast(EFEAT)).then_inc(flags_in[n], 16)
                    rows = tile_rows(s, P)
                    if isinstance(s, int) and s == STEPS - 1:
                        rows = tile_rows(s, LAST_PARTS)
                    sp.dma_start(node_rows[rows, 0, :], x[rows, :]).then_inc(x_out[0], 16)

            sp.wait_ge(idx_kept, 4)
            sp.wait_ge(flags_out, 32)
            l0_step(0, first=True)
            l0_step(1)
            with sp.Fori(2, STEPS - 1) as s:
                l0_step(s)
            l0_step(STEPS - 1)
            l0_step(STEPS)
            sp.dma_start(node_rows[NODES:N_PAD, 0, :], x[0:N_PAD - NODES, :]).then_inc(x_out[1], 16)

            sp.wait_ge(g_idx_ready, 1)
            sp.wait_ge(dst_kept, GROUPS)
            sp.wait_ge(x_out[0], 16 * STEPS)
            sp.wait_ge(x_out[1], 16)
            for n in range(PER):
                sp.wait_ge(scattered[n], 16 * TILES * STEPS)

            def l1_step(s, first=False):
                last = isinstance(s, int) and s == STEPS
                if not last:
                    if not first:
                        sp.wait_ge(l1_gathered, s * 16 * STEP_CHUNKS)
                    for n in range(PER):
                        load_idx(idx_in, dst_idx, s, n, l1_in_idx)
                    if not first:
                        sp.wait_ge(y_ready, s)
                    sp.dma_start(near[:, STEP_CHUNKS:, :, :],
                                 node_rows[tile_rows(s)].rearrange("(p c) t f -> p c t f", p=P)).then_inc(tile_in, 16)
                if not first:
                    if not (isinstance(s, int) and s == 1):
                        sp.wait_ge(l1_scattered, (s - 1) * 16 * STEP_CHUNKS)
                    for n in range(PER):
                        load_idx(idx_out, g_idx, s - 1, n, l1_out_idx)
                if not last:
                    for n in range(PER):
                        if not first:
                            sp.wait_ge(aggr_ready, (s - 1) * PER + n + 1)
                        load_flags(s, n, l1_flags_in)
                if not first:
                    sp.wait_ge(x1_ready, s)
                    sp.dma_start(x1_table[tile_rows(s - 1), :].rearrange("(p c) f -> p c f", p=P),
                                 x1[:, STEP_CHUNKS:, :]).then_inc(x1_out, 16)

            for n in range(PER):
                sp.wait_ge(summed, GROUPS)
            l1_step(0, first=True)
            l1_step(1)
            with sp.Fori(2, STEPS) as s:
                l1_step(s)
            l1_step(STEPS)

            sp.wait_ge(l1_scattered, 16 * STEP_CHUNKS * STEPS)
            sp.wait_ge(x1_out, 16 * STEPS)

            def load_tile(t, n):
                sp.dma_start(in_x1[n], x1_table[tile_rows(t), :].rearrange("(p c) f -> p c f", p=P)).then_inc(z_in[n], 16)
                sp.dma_start(in_g[n], g_table[tile_rows(t), :].rearrange("(p c) f -> p c f", p=P)).then_inc(z_in[n], 16)

            load_tile(0, 0)
            load_tile(1, 1)
            with sp.Fori(1, STEPS // 2) as i:
                for n in range(2):
                    sp.wait_ge(z_added, (i - 1) * 2 + n + 1)
                    load_tile(i * 2 + n, n)
            sp.wait_ge(z_added, STEPS - 2)
            load_tile(STEPS - 1, 0)

        @block.gpsimd
        def _(pool):
            pool.iota(pair_i[:], pattern=[[1, PAIR_COLS], [0, 2]], base=0,
                      channel_multiplier=PAIR_COLS).then_inc(pair_iota, 1)
            pool.iota(part_i[:], pattern=[[0, 1]], base=0, channel_multiplier=1).then_inc(part_iota, 1)
            pool.memset(ident[:], 0.0).then_inc(ident_zero, 1)
            pool.wait_ge(ident_zero, 1)
            pool.affine_select(out=ident[:], in_=ident[:], compare_op=ALU.not_equal, fill=1.0, base=0,
                               pattern=[[-1, P]], channel_multiplier=1).then_inc(ident_done, 1)

            def gather(n, target, table, top, ready):
                pool.sem_inc(pool_stands, 1)
                for t in range(TILES):
                    pool.indirect_dma_start(out=target(t), out_offset=None, in_=table,
                                            in_offset=bass.IndirectOffsetOnAxis(ap=idx_in[n][:, t:t + 1], axis=0),
                                            bounds_check=top, oob_is_err=False).then_inc(ready, 16)

            def scatter(n, source, table, top, ready):
                pool.sem_inc(pool_stands, 1)
                for t in range(TILES):
                    pool.indirect_dma_start(out=table, in_=source(t), in_offset=None,
                                            out_offset=bass.IndirectOffsetOnAxis(ap=idx_out[n][:, t:t + 1], axis=0),
                                            bounds_check=top, oob_is_err=False).then_inc(ready, 16)

            def l0_gather(s, first=False):
                for n in range(PER):
                    pool.wait_ge(in_idx[n], (s + 1) * 16)
                    if not first:
                        pool.wait_ge(attrs_turned, (s - 1) * PER + n + 1)
                        pool.wait_ge(dst_kept, (s - 1) * PER + n + 1)
                    gather(n, lambda t, n=n: pairs[n][:, t, :], edge_pairs, EDGES // 2 - 1, gathered[n])

            def l0_scatter(s):
                for n in range(PER):
                    pool.wait_ge(out_idx[n], (s + 1) * 16)
                    pool.wait_ge(delta_ready, s * PER + n + 1)
                    scatter(n, lambda t, n=n: delta[n][:, t, :], node_halves, 2 * N_PAD - 1, scattered[n])

            pool.wait_ge(pairs_out, 16)
            l0_gather(0, first=True)
            l0_gather(1)
            for n in range(2):
                pool.wait_ge(c0_out[n], 16 * ((STEPS + 1 - n) // 2))
            l0_scatter(0)
            with pool.Fori(2, STEPS) as s:
                l0_gather(s)
                l0_scatter(s - 1)
            l0_scatter(STEPS - 1)

            for n in range(PER):
                pool.wait_ge(scattered[n], 16 * TILES * STEPS)
            pool.wait_ge(x_out[0], 16 * STEPS)

            def l1_gather(s, first=False):
                if not first:
                    pool.wait_ge(y_ready, s)
                for n in range(PER):
                    pool.wait_ge(l1_in_idx[n], (s + 1) * 16)
                    gather(n, lambda t, n=n: near[:, n * TILES + t, :, :].rearrange("p t f -> p (t f)"),
                           node_pairs, N_PAD - 1, l1_gathered)

            def l1_scatter(s):
                pool.wait_ge(g_ready, s + 1)
                for n in range(PER):
                    pool.wait_ge(l1_out_idx[n], (s + 1) * 16)
                    scatter(n, lambda t, n=n: delta[n][:, t, :], g_table, N_PAD - 1, l1_scattered)

            l1_gather(0, first=True)
            l1_gather(1)
            pool.wait_ge(g0_out, 16 * STEPS)
            l1_scatter(0)
            with pool.Fori(2, STEPS) as s:
                l1_gather(s)
                l1_scatter(s - 1)
            l1_scatter(STEPS - 1)

        @block.scalar
        def _(act):
            act.wait_ge(attr_in, 32)
            act.wait_ge(dst_in, 16)
            act.activation(pair_tile[0:EDGE_PARTS, :, :, EFEAT],
                           dst_i[0:EDGE_PARTS, :].rearrange("p (q t) -> p q t", t=2), ACT.Copy).then_inc(pair_ids, 1)
            act.wait_ge(src_in, 16)
            act.activation(pair_tile[0:EDGE_PARTS, :, :, EFEAT + 1],
                           src_i[0:EDGE_PARTS, :].rearrange("p (q t) -> p q t", t=2), ACT.Copy).then_inc(pair_ids, 1)
            act.wait_ge(weights_in, 16 * 9)
            act.activation(g0_relu[:], b_b[:], ACT.Relu).then_inc(g0_relu_done, 1)

            for n in range(2 * (LEVELS - ROW_LEVELS)):
                act.wait_ge(turned, n + 1)
                to = KT[0] if n % 2 == 0 else K[0]
                act.activation(to[:], p_turn[n % 2][:], ACT.Copy).then_inc(untangled, 1)

            act.wait_ge(setup, 3)
            act.dma_start(words[0:1].rearrange("(a c) -> a c", a=1), sentinel[:]).then_inc(words_out, 16)
            act.dma_start(words[P * COLS + 1:P * COLS + 2].rearrange("(a c) -> a c", a=1), sentinel[:]).then_inc(words_out, 16)
            act.wait_ge(sort_done, 1)
            act.dma_start(words[1:P * COLS + 1].rearrange("(p c) -> p c", p=P), K[1][:]).then_inc(words_out, 16)
            act.wait_ge(words_out, 48)
            act.dma_start(prev[:], words[0:P * COLS].rearrange("(p c) -> p c", p=P)).then_inc(near_words, 16)
            act.dma_start(nxt[:], words[2:P * COLS + 2].rearrange("(p c) -> p c", p=P)).then_inc(near_words, 16)
            act.wait_ge(tables, 1)
            act.dma_start(flags[0, :].rearrange("(p c) -> p c", p=P), same[:]).then_inc(flags_out, 16)
            act.dma_start(flags[1, :].rearrange("(p c) -> p c", p=P), floor_f[:]).then_inc(flags_out, 16)
            for n, to in enumerate((pair_idx, row_idx, node_at, twin_at)):
                act.wait_ge(idx_turned, n + 1)
                turned_v = p_turn[n % 2][:].rearrange("p (t g) -> p g t", t=TILES)
                act.activation(to[:], turned_v[:, 0:GROUPS, :], ACT.Copy).then_inc(idx_kept, 1)

            def l0_hidden(s, first=False):
                for n in range(PER):
                    act.wait_ge(hid_psum, s * PER + n + 1)
                    if not first:
                        act.wait_ge(delta_psum, (s - 1) * PER + n + 1)
                    act.activation(hidden[n][:], p_hid[n][:], ACT.Relu, bias=c1[:, 0:1]).then_inc(hid_ready, 1)
                act.dma_start(g_table[tile_rows(s), :].rearrange("(p c) f -> p c f", p=P), g0_tile[:]).then_inc(g0_out, 16)

            act.wait_ge(g0_ready, 1)
            act.wait_ge(c1_ready, 1)
            l0_hidden(0, first=True)
            with act.Fori(1, STEPS) as s:
                l0_hidden(s)

            def l1_scalar(s):
                act.wait_ge(yc_ready, s + 1)
                act.activation(ysq[:], yc[:], ACT.Square).then_inc(ysq_ready, 1)
                act.wait_ge(yvar_ready, s + 1)
                act.activation(ystd[:], yvar[:], ACT.Sqrt, bias=eps[:, 0:1], scale=1.0 / FEAT).then_inc(ystd_ready, 1)
                act.wait_ge(gz_ready, s + 1)
                act.activation(gr[:], gz[:], ACT.Relu).then_inc(gr_ready, 1)

            with act.Fori(0, STEPS) as s:
                l1_scalar(s)

            def square(t, n):
                act.wait_ge(z_added, t + 1)
                act.activation(zsq[n], z[n], ACT.Square).then_inc(z_squared, 1)

            def deviation(t, n):
                act.wait_ge(zvar_ready, t + 1)
                act.activation(zstd[n][:], zvar[n][:], ACT.Sqrt, bias=eps[:, 0:1], scale=1.0 / FEAT).then_inc(zstd_ready, 1)

            def store(t, n, parts=P):
                act.wait_ge(z_done, t + 1)
                act.dma_start(out[tile_rows(t, parts), :].rearrange("(p c) f -> p c f", p=parts),
                              z_out[n][0:parts]).then_inc(out_done[n], 16)

            square(0, 0)
            square(1, 1)
            deviation(0, 0)
            with act.Fori(1, STEPS // 2) as i:
                for n in range(2):
                    square(i * 2 + n, n)
                    deviation(i * 2 + n - 1, 1 - n)
                    store(i * 2 + n - 2, n)
            t = STEPS - 1
            square(t, 0)
            deviation(t - 1, 1)
            store(t - 2, 0)
            deviation(t, 0)
            store(t - 1, 1)
            store(t, 0, LAST_PARTS)
            act.wait_ge(out_done[0], 16 * (STEPS // 2 + 1))
            act.wait_ge(out_done[1], 16 * (STEPS // 2))

        @block.tensor
        def _(pe):
            pe.wait_ge(c1_relu_ready, 1)
            pe.matmul(p_rows[:, 0, 0, :], c1_relu[:], w2[:], start=True, stop=True).then_inc(c0_psum, 1)
            pe.wait_ge(ident_done, 1)
            pe.wait_ge(weights_in, 16 * 9)
            pe.transpose(p_hid[0][0:FEAT, 0:FEAT], w_in[:], ident[0:FEAT, 0:FEAT]).then_inc(w_turned, 1)
            for n in range(2 * (LEVELS - ROW_LEVELS)):
                pe.wait_ge(turn_ready, n + 1)
                if n % 2:
                    from_ = KT[(n // 2 + 1) % 2]
                else:
                    from_ = K[1 if n == 0 else 0]
                for t in range(TILES):
                    ins = pe.transpose(p_turn[n % 2][:, t * P:(t + 1) * P], from_[:, t * P:(t + 1) * P], ident[:])
                ins.then_inc(turned, 1)
            pe.wait_ge(tables, 1)
            for n, from_ in enumerate((pair_f, row_f, node, twin)):
                if n >= 2:
                    pe.wait_ge(idx_kept, n - 1)
                for t in range(TILES):
                    ins = pe.transpose(p_turn[n % 2][:, t * P:(t + 1) * P], from_[:, t * P:(t + 1) * P], ident[:])
                ins.then_inc(idx_turned, 1)

            def l0_turn(s, n, first=False):
                pe.wait_ge(edge_picked, s * PER + n + 1)
                if not first:
                    pe.wait_ge(maxed, (s - 1) * PER + n + 1)
                for t in range(TILES):
                    ins = pe.transpose(p_feat[n][0:EFEAT, t * P:(t + 1) * P], pairs[n][:, t, 0:EFEAT], ident[:])
                ins.then_inc(attrs_turned, 1)

            def l0_mlp_in(s, n, first=False):
                pe.wait_ge(averaged, s * PER + n + 1)
                if not first:
                    pe.wait_ge(hid_ready, (s - 1) * PER + n + 1)
                pe.matmul(p_hid[n][:], w1[:], feats[n][:], start=True, stop=True).then_inc(hid_psum, 1)

            def l0_mlp_out(s, n, first=False):
                pe.wait_ge(hid_ready, s * PER + n + 1)
                if not first:
                    pe.wait_ge(delta_ready, (s - 1) * PER + n + 1)
                for t in range(TILES):
                    ins = pe.matmul(p_rows[:, n, t, :], hidden[n][:, t * P:(t + 1) * P], w2[:],
                                    start=True, stop=True)
                ins.then_inc(delta_psum, 1)

            def l0_pe(s, first=False):
                l0_turn(s, 0, first)
                l0_mlp_in(s, 0, first)
                l0_turn(s, 1, first)
                l0_mlp_out(s, 0, first)
                l0_mlp_in(s, 1, first)
                l0_mlp_out(s, 1, first)

            pe.wait_ge(ones_done, 2)
            pe.wait_ge(weights_in, 16 * 9)
            pe.wait_ge(setup, 3)
            pe.wait_ge(c0_ready, 1)
            pe.wait_ge(w_t_ready, 1)
            l0_pe(0, first=True)
            with pe.Fori(1, STEPS) as s:
                l0_pe(s)

            def l1_pe(s, first=False):
                pe.wait_ge(x1_ready, s + 1)
                for n in range(PER):
                    if not first:
                        pe.wait_ge(aggr_ready, (s - 1) * PER + n + 1)
                    pe.sem_inc(pe_stands, 1)
                    for t in range(TILES):
                        ins = pe.transpose(p_feat[n][:, t * P:(t + 1) * P], x1[:, n * TILES + t, :], ident[:])
                    ins.then_inc(x1_turned, 1)
                for n in range(PER):
                    pe.wait_ge(aggr_ready, s * PER + n + 1)
                    if not first and n == 0:
                        pe.wait_ge(gz_ready, s)
                    for t in range(TILES):
                        ins = pe.matmul(p_rows[:, n, t, :], aggr[n][:, t * P:(t + 1) * P], w_t[:],
                                        start=True, stop=True)
                    ins.then_inc(g_psum, 1)

            pe.wait_ge(delta_ready, GROUPS)
            l1_pe(0, first=True)
            with pe.Fori(1, STEPS) as s:
                l1_pe(s)

        @block.vector
        def _(dve):
            steps = [0]

            def link(ins):
                steps[0] += 1
                ins.then_inc(sorting, 1)
                dve.wait_ge(sorting, steps[0])

            def mark(ins):
                steps[0] += 1
                ins.then_inc(sorting, 1)

            for n in range(PER):
                dve.memset(p_feat[n][EFEAT:2 * EFEAT, :], 1.0).then_inc(ones_done, 1)
            dve.memset(w1[EFEAT:2 * EFEAT, :], 0.0).then_inc(setup, 1)
            mark(dve.memset(feats[1][:, COLS - 1:COLS], 0.0))
            mark(dve.memset(aggr[1][:, COLS - 1:COLS], 0.0))
            dve.memset(eps[:], EPS).then_inc(setup, 1)
            dve.memset(sentinel[:], PAD).then_inc(setup, 1)
            link(dve.memset(K[0][:], PAD))
            q = slice(0, EDGE_PARTS)
            dve.wait_ge(src_in, 16)
            link(dve.tensor_copy(src_f[q, :], src_i[q, :]))
            link(dve.tensor_scalar(high[q, :], src_f[q, :], float(HALF), float(SIGN_CODE - HALF), ALU.is_ge, ALU.mult))
            link(dve.scalar_tensor_tensor(out=code_i[q, :], in0=src_f[q, :], scalar=float(CODE0), in1=high[q, :],
                                          op0=ALU.add, op1=ALU.add))
            link(dve.tensor_scalar(code_s[q, :], code_i[q, :], PAIR_BITS, None, ALU.logical_shift_left))
            dve.wait_ge(pair_iota, 1)
            link(dve.tensor_tensor(K[0][q, 0:EDGE_COLS].bitcast(I32), code_s[q, :], pair_i[q, :], ALU.bitwise_or))
            dve.wait_ge(weights_in, 16 * 9)
            dve.tensor_scalar(c1[:], w1_u[:], u0[:, 0:1], b1_c[:, 0:1], ALU.mult, ALU.add).then_inc(c1_ready, 1)
            dve.wait_ge(c1_ready, 1)
            dve.tensor_scalar(c1_relu[:], c1[:, 0:1].broadcast_to([HID, P]), 0.0, None, ALU.max).then_inc(c1_relu_ready, 1)
            dve.wait_ge(g0_relu_done, 1)
            link(dve.tensor_reduce(g0_sum[:], g0_relu[:], AX_X, ALU.add))
            link(dve.tensor_scalar(g0_sum[:], g0_sum[:], 1.0 / FEAT, None, ALU.mult))
            link(dve.tensor_scalar(g0_row[:], g0_relu[:], g0_sum[:, 0:1], None, ALU.subtract))
            dve.tensor_copy(g0_tile[:], g0_row[:].unsqueeze(1).broadcast_to([P, TROWS, FEAT])).then_inc(g0_ready, 1)
            dve.wait_ge(c0_psum, 1)
            dve.tensor_tensor(c0_tile[:], p_rows[:, 0, 0:1, :].broadcast_to([P, TROWS, FEAT]),
                              b2_b[:].unsqueeze(1).broadcast_to([P, TROWS, FEAT]), ALU.add).then_inc(c0_ready, 1)
            dve.wait_ge(w_turned, 1)
            dve.tensor_copy(w_t[:], p_hid[0][0:FEAT, 0:FEAT]).then_inc(w_t_ready, 1)
            dve.wait_ge(part_iota, 1)
            for bit in range(8):
                mark(dve.tensor_scalar(bit_a[:, bit:bit + 1], part_i[:], bit, None, ALU.logical_shift_right))
            dve.wait_ge(sorting, steps[0])
            link(dve.tensor_scalar(bit_b[:], bit_a[:], 1, None, ALU.bitwise_and))
            link(dve.tensor_scalar(sign[:], bit_b[:], -2.0, 1.0, ALU.mult, ALU.add))
            link(dve.tensor_tensor(flip[:, 0:7], sign[:, 0:7], sign[:, 1:8], ALU.mult))
            link(dve.tensor_scalar(K[1][:], K[0][:], sign[:, 0:1], None, ALU.mult))

            def exchange(bufs, cur, dist, mirrored=False, ends_phase=None):
                a = bufs[cur][:].rearrange("p (a t d) -> p a t d", t=2, d=dist)
                o = bufs[1 - cur][:].rearrange("p (a t d) -> p a t d", t=2, d=dist)
                left, right = a[:, :, 0, :], a[:, :, 1, :]
                back = slice(None, None, -1) if mirrored and dist > 1 else slice(None)
                dve.tensor_tensor(o[:, :, 0, :], left, right[:, :, back], ALU.min)
                ins = dve.tensor_tensor(o[:, :, 1, :], right, left[:, :, back], ALU.max)
                if ends_phase is not None:
                    ins.then_inc(ends_phase, 1)
                else:
                    link(ins)
                return 1 - cur

            cur = 1
            for level in range(1, ROW_LEVELS + 1):
                cur = exchange(K, cur, 2 ** (level - 1), mirrored=True)
                for d in range(level - 2, -1, -1):
                    cur = exchange(K, cur, 2 ** d)
            for level in range(ROW_LEVELS + 1, LEVELS + 1):
                m = level - ROW_LEVELS - 1
                dve.tensor_scalar(K[1 - cur][:], K[cur][:], flip[:, m:m + 1], None, ALU.mult).then_inc(turn_ready, 1)
                dve.wait_ge(untangled, 2 * m + 1)
                cur = 0
                for d in range(m, -1, -1):
                    cur = exchange(KT, cur, 2 ** d, ends_phase=turn_ready if d == 0 else None)
                dve.wait_ge(untangled, 2 * m + 2)
                cur = 0
                for d in range(ROW_LEVELS - 1, -1, -1):
                    cur = exchange(K, cur, 2 ** d, ends_phase=sort_done if d == 0 and level == LEVELS else None)
            dve.wait_ge(sort_done, 1)

            here = K[1]
            link(dve.tensor_scalar(code_here[:], here[:].bitcast(I32), PAIR_BITS, None, ALU.logical_shift_right))
            link(dve.tensor_scalar(pair_bits[:], here[:].bitcast(I32), 2 ** PAIR_BITS - 1, None, ALU.bitwise_and))
            mark(dve.tensor_copy(pair_f[:], pair_bits[:]))
            link(dve.tensor_scalar(upper[:], code_here[:], float(SIGN_CODE), float(HALF - SIGN_CODE), ALU.is_ge, ALU.mult))
            link(dve.scalar_tensor_tensor(out=node[:], in0=code_here[:], scalar=float(-CODE0), in1=upper[:],
                                          op0=ALU.add, op1=ALU.add))
            dve.wait_ge(near_words, 32)
            mark(dve.tensor_scalar(code_prev[:], prev[:].bitcast(I32), PAIR_BITS, None, ALU.logical_shift_right))
            link(dve.tensor_scalar(code_next[:], nxt[:].bitcast(I32), PAIR_BITS, None, ALU.logical_shift_right))
            mark(dve.tensor_tensor(same[:], code_here[:], code_prev[:], ALU.is_equal))
            mark(dve.tensor_tensor(ends[:], code_here[:], code_next[:], ALU.is_equal))
            link(dve.tensor_tensor(twin[:], here[:], prev[:], ALU.is_equal))
            link(dve.tensor_scalar(floor_f[:], same[:], 2.0, -1.0, ALU.mult, ALU.add))
            link(dve.tensor_scalar(floor_f[:], floor_f[:], FLT_MAX, None, ALU.mult))
            link(dve.tensor_scalar(skip[:], ends[:], SKIP, 1.0, ALU.mult, ALU.add))
            dve.scalar_tensor_tensor(out=row_f[:], in0=node[:], scalar=2.0, in1=skip[:],
                                     op0=ALU.mult, op1=ALU.add).then_inc(tables, 1)

            def l0_pick(s, n):
                g = s * PER + n
                at = group_of(s, n)
                dve.wait_ge(gathered[n], (s + 1) * 16 * TILES)
                dve.tensor_tensor(wrong[n][:], pairs[n][:, :, EFEAT + 1], node_at[:, at, :].rearrange("p a t -> p (a t)"),
                                  ALU.not_equal).then_inc(edge_known, 1)
                dve.wait_ge(edge_known, g + 1)
                dve.tensor_tensor(odd[n][:], wrong[n][:], twin_at[:, at, :].rearrange("p a t -> p (a t)"),
                                  ALU.max).then_inc(edge_odd, 1)
                dve.wait_ge(edge_odd, g + 1)
                dve.sem_inc(dve_stands, 1)
                dve.copy_predicated(out=pairs[n][:, :, 0:HALF_ROW], mask=odd[n][:].unsqueeze(2).broadcast_to([P, TILES, HALF_ROW]),
                                    data=pairs[n][:, :, HALF_ROW:PAIR_ROW]).then_inc(edge_picked, 1)
                dve.wait_ge(edge_picked, g + 1)
                dve.tensor_copy(dst_idx[:, at, :].rearrange("p a t -> p (a t)"), pairs[n][:, :, EFEAT]).then_inc(dst_kept, 1)

            def l0_scan(s, n, first=False):
                g = s * PER + n
                dve.wait_ge(attrs_turned, g + 1)
                dve.wait_ge(flags_in[n], (s + 1) * 32)
                if not first:
                    dve.wait_ge(hid_psum, (s - 1) * PER + n + 1)
                if not (first and n == 0):
                    dve.wait_ge(maxed, g)
                dve.tensor_tensor_scan(feats[n][0:2 * EFEAT, :], same_b[n][:], p_feat[n][:],
                                       feats[1 - n][0:2 * EFEAT, COLS - 1:COLS], ALU.mult, ALU.add).then_inc(summed, 1)
                dve.tensor_tensor_scan(feats[n][2 * EFEAT:3 * EFEAT, :], floor_b[n][:], p_feat[n][0:EFEAT, :],
                                       feats[1 - n][2 * EFEAT:3 * EFEAT, COLS - 1:COLS], ALU.min, ALU.max).then_inc(maxed, 1)
                dve.wait_ge(summed, g + 1)
                dve.reciprocal(count_r[n][:], feats[n][EFEAT:2 * EFEAT, :]).then_inc(inverted, 1)
                dve.wait_ge(inverted, g + 1)
                dve.tensor_tensor(feats[n][3 * EFEAT:4 * EFEAT, :], feats[n][0:EFEAT, :], count_r[n][:],
                                  ALU.mult).then_inc(averaged, 1)

            def l0_delta(s, n, first=False):
                dve.wait_ge(delta_psum, s * PER + n + 1)
                if not first:
                    dve.wait_ge(scattered[n], s * 16 * TILES)
                dve.tensor_tensor(delta[n][:], p_rows[:, n, :, :],
                                  b2_b[:].unsqueeze(1).broadcast_to([P, TILES, FEAT]), ALU.add).then_inc(delta_ready, 1)

            def l0_dve(s, first=False):
                for n in range(PER):
                    l0_pick(s, n)
                    l0_scan(s, n, first)
                for n in range(PER):
                    l0_delta(s, n, first)

            dve.wait_ge(idx_kept, 4)
            l0_dve(0, first=True)
            with dve.Fori(1, STEPS) as s:
                l0_dve(s)

            dve.tensor_scalar(g_idx[:], row_idx[:], -1.0, 0.5, ALU.add, ALU.mult).then_inc(g_idx_ready, 1)

            inv = 1.0 / FEAT

            def rows_b(a, rows=LN_ROWS):
                return a[:].unsqueeze(2).broadcast_to([P, rows, FEAT])

            def l1_dve(s, first=False):
                dve.wait_ge(l1_gathered, (s + 1) * 16 * STEP_CHUNKS)
                dve.wait_ge(tile_in, (s + 1) * 16)
                dve.tensor_tensor(y[:], near[:, :, 0, :], near[:, :, 1, :], ALU.add).then_inc(y_ready, 1)
                dve.wait_ge(y_ready, s + 1)
                dve.tensor_reduce(ysum[:], y[:], AX_X, ALU.add).then_inc(ysum_ready, 1)
                dve.wait_ge(ysum_ready, s + 1)
                dve.tensor_scalar(ymean[:], ysum[:], inv, None, ALU.mult).then_inc(ymean_ready, 1)
                dve.wait_ge(ymean_ready, s + 1)
                dve.tensor_tensor(yc[:], y[:], rows_b(ymean), ALU.subtract).then_inc(yc_ready, 1)
                dve.wait_ge(ysq_ready, s + 1)
                dve.tensor_reduce(yvar[:], ysq[:], AX_X, ALU.add).then_inc(yvar_ready, 1)
                dve.wait_ge(ystd_ready, s + 1)
                dve.reciprocal(yrstd[:], ystd[:]).then_inc(yrstd_ready, 1)
                dve.wait_ge(yrstd_ready, s + 1)
                if not first:
                    dve.wait_ge(x1_turned, s * PER)
                    dve.wait_ge(x1_out, s * 16)
                dve.tensor_tensor(x1[:], yc[:], rows_b(yrstd), ALU.mult).then_inc(x1_ready, 1)
                for n in range(PER):
                    g = s * PER + n
                    dve.wait_ge(x1_turned, g + 1)
                    dve.wait_ge(l1_flags_in[n], (s + 1) * 16)
                    if not first:
                        dve.wait_ge(g_psum, (s - 1) * PER + n + 1)
                    if not (first and n == 0):
                        dve.wait_ge(aggr_ready, g)
                    dve.tensor_tensor_scan(aggr[n][:], same_b[n][:], p_feat[n][:], aggr[1 - n][:, COLS - 1:COLS],
                                           ALU.mult, ALU.add).then_inc(aggr_ready, 1)
                dve.wait_ge(g_psum, (s + 1) * PER)
                dve.tensor_tensor(gz[:].rearrange("p (n t) f -> p n t f", n=PER), p_rows,
                                  b_b[:].unsqueeze(1).unsqueeze(1).broadcast_to([P, PER, TILES, FEAT]),
                                  ALU.add).then_inc(gz_ready, 1)
                dve.wait_ge(gr_ready, s + 1)
                dve.tensor_reduce(gsum[:], gr[:], AX_X, ALU.add).then_inc(gsum_ready, 1)
                dve.wait_ge(gsum_ready, s + 1)
                dve.tensor_scalar(gmean[:], gsum[:], inv, None, ALU.mult).then_inc(gmean_ready, 1)
                dve.wait_ge(gmean_ready, s + 1)
                if not first:
                    dve.wait_ge(l1_scattered, s * 16 * STEP_CHUNKS)
                for n in range(PER):
                    ins = dve.tensor_tensor(delta[n][:], gr[:, n * TILES:(n + 1) * TILES, :],
                                            gmean[:, n * TILES:(n + 1) * TILES].unsqueeze(2).broadcast_to([P, TILES, FEAT]),
                                            ALU.subtract)
                ins.then_inc(g_ready, 1)

            for n in range(PER):
                dve.wait_ge(scattered[n], 16 * TILES * STEPS)
            l1_dve(0, first=True)
            with dve.Fori(1, STEPS) as s:
                l1_dve(s)

            def add(t, n, first=False):
                dve.wait_ge(z_in[n], (t // 2 + 1) * 32 if isinstance(t, int) else (t + (2 - n)) * 16)
                dve.tensor_tensor(z[n], in_x1[n], in_g[n], ALU.add).then_inc(z_added, 1)

            def variance(t, n):
                dve.wait_ge(z_squared, t + 1)
                dve.tensor_reduce(zvar[n][:], zsq[n], AX_X, ALU.add).then_inc(zvar_ready, 1)
                dve.wait_ge(zstd_ready, t + 1)
                dve.reciprocal(zrstd[n][:], zstd[n][:]).then_inc(zrstd_ready, 1)
                dve.wait_ge(zrstd_ready, t + 1)

            def scale(t, n, first=False):
                if not first:
                    dve.wait_ge(out_done[n], (t // 2) * 16 if isinstance(t, int) else (t - n) * 8)
                dve.tensor_tensor(z_out[n], z[n], rows_b(zrstd[n], TROWS), ALU.mult).then_inc(z_done, 1)

            add(0, 0)
            add(1, 1)
            variance(0, 0)
            scale(0, 0, first=True)
            dve.wait_ge(z_done, 1)
            add(2, 0)
            variance(1, 1)
            scale(1, 1, first=True)
            dve.wait_ge(z_done, 2)
            add(3, 1)
            variance(2, 0)
            scale(2, 0)
            with dve.Fori(2, STEPS // 2) as i:
                for n in range(2):
                    dve.wait_ge(z_done, i * 2 + n - 1)
                    dve.wait_ge(z_in[n], (i + 1) * 32)
                    dve.tensor_tensor(z[n], in_x1[n], in_g[n], ALU.add).then_inc(z_added, 1)
                    variance(i * 2 + n - 1, 1 - n)
                    dve.wait_ge(out_done[1 - n], (i - 1 + n) * 16)
                    dve.tensor_tensor(z_out[1 - n], z[1 - n], rows_b(zrstd[1 - n], TROWS), ALU.mult).then_inc(z_done, 1)
            dve.wait_ge(z_done, STEPS - 2)
            add(STEPS - 1, 0)
            variance(STEPS - 2, 1)
            scale(STEPS - 2, 1)
            variance(STEPS - 1, 0)
            scale(STEPS - 1, 0)


_INS = ["x", "src", "dst", "edge_attr_32", "L0_gnn_u", "L0_gnn_W1", "L0_gnn_b1", "L0_gnn_W2", "L0_gnn_b2", "L1_gnn_W", "L1_gnn_b"]


def kernel(**inputs):
    import numpy as _np
    import concourse.bacc as _bacc
    from concourse import mybir as _mybir
    from concourse.bass_utils import run_bass_kernel_spmd as _run

    nc = _bacc.Bacc("TRN2", target_bir_lowering=False, num_devices=1)
    arrays, args = {}, []
    for name in _INS:
        a = _np.ascontiguousarray(inputs[name])
        arrays[f"in_{name}"] = a
        args.append(nc.dram_tensor(f"in_{name}", a.shape, _mybir.dt.from_np(a.dtype), kind="ExternalInput").ap())
    args.append(nc.dram_tensor("out_0", (NODES, FEAT), F32, kind="ExternalOutput").ap())
    gnn_kernel(nc, *args)
    r = _run(nc, [arrays], core_ids=[0])
    return r.results[0]["out_0"]
```

```python
from contextlib import ExitStack

import numpy as np

import concourse.bass as bass
from concourse import mybir

ALU = mybir.AluOpType
ACT = mybir.ActivationFunctionType
AX_X = mybir.AxisListType.X
F32 = mybir.dt.float32
I32 = mybir.dt.int32

P = 128
NODES, FEAT = 100000, 64
EDGES, EFEAT = 50000, 32
HID = 128
EPS = 1e-5
FLT_MAX = float(np.finfo(np.float32).max)

COLS = 512
LEVELS = 16
ROW_LEVELS = 9
EDGE_PARTS = 125
EDGE_COLS = EDGES // EDGE_PARTS
PAIR_COLS = EDGE_COLS // 2
HALF = NODES // 2
CODE0 = 30 * 256
SIGN_CODE = 65536
PAIR_BITS = 15
PAD = 2.0 ** 120
SKIP = 262144.0

TILES = COLS // P
GROUPS = 98
PER = 2
STEPS = GROUPS // PER
CHUNKS = GROUPS * TILES
STEP_CHUNKS = PER * TILES
PAIR_ROW = 2 * (EFEAT + 2)
HALF_ROW = EFEAT + 2

TROWS = 16
TILE = P * TROWS
N_PAD = STEPS * TILE
LAST = NODES - (STEPS - 1) * TILE
LAST_PARTS = LAST // TROWS
LN_ROWS = STEP_CHUNKS + TROWS
assert N_PAD >= NODES and LAST_PARTS * TROWS == LAST and GROUPS * COLS >= EDGES

C0_EARLY = 29


def gnn_kernel(nc, x, src, dst, edge_attr, u, W1, b1, W2, b2, W, b, out):
    edge_pairs = nc.dram_tensor("edge_pairs", (EDGES // 2, PAIR_ROW), F32, kind="Internal").ap()
    node_rows = nc.dram_tensor("node_rows", (N_PAD, 2, FEAT), F32, kind="Internal").ap()
    x1_table = nc.dram_tensor("x1_table", (N_PAD, FEAT), F32, kind="Internal").ap()
    g_table = nc.dram_tensor("g_table", (N_PAD, FEAT), F32, kind="Internal").ap()
    words = nc.dram_tensor("words", (P * COLS + 2,), F32, kind="Internal").ap()
    flags = nc.dram_tensor("flags", (3, P * COLS), F32, kind="Internal").ap()

    node_halves = node_rows.rearrange("n t f -> (n t) f")
    node_pairs = node_rows.rearrange("n t f -> n (t f)")

    with ExitStack() as ctx:
        def sb(name, shape, dt=F32):
            return ctx.enter_context(nc.sbuf_tensor(name, shape, dt))

        def ps(name, shape):
            return ctx.enter_context(nc.psum_tensor(name, shape, F32))

        def sem(name):
            return ctx.enter_context(nc.semaphore(name))

        src_i = sb("src_i", [P, EDGE_COLS], I32)
        dst_i = sb("dst_i", [P, EDGE_COLS], I32)
        src_f = sb("src_f", [P, EDGE_COLS])
        high = sb("high", [P, EDGE_COLS])
        code_i = sb("code_i", [P, EDGE_COLS], I32)
        code_s = sb("code_s", [P, EDGE_COLS], I32)
        pair_i = sb("pair_i", [P, EDGE_COLS], I32)
        pair_tile = sb("pair_tile", [P, PAIR_COLS, 2, HALF_ROW])
        K = [sb(f"K{n}", [P, COLS]) for n in range(2)]
        KT = [sb(f"KT{n}", [P, COLS]) for n in range(2)]
        part_i = sb("part_i", [P, 1], I32)
        bit_a = sb("bit_a", [P, 8], I32)
        bit_b = sb("bit_b", [P, 8], I32)
        sign = sb("sign", [P, 8])
        flip = sb("flip", [P, 8])
        ident = sb("ident", [P, P])
        prev = sb("prev", [P, COLS])
        nxt = sb("nxt", [P, COLS])
        code_here = sb("code_here", [P, COLS], I32)
        code_prev = sb("code_prev", [P, COLS], I32)
        code_next = sb("code_next", [P, COLS], I32)
        pair_bits = sb("pair_bits", [P, COLS], I32)
        same = sb("same", [P, COLS])
        ends = sb("ends", [P, COLS])
        floor_f = sb("floor_f", [P, COLS])
        pair_f = sb("pair_f", [P, COLS])
        twin = sb("twin", [P, COLS])
        upper = sb("upper", [P, COLS])
        node = sb("node", [P, COLS])
        skip = sb("skip", [P, COLS])
        row_f = sb("row_f", [P, COLS])
        sentinel = sb("sentinel", [1, 1])
        one = sb("one", [P, 1])
        count = sb("count", [P, COLS])
        whole = sb("whole", [P, 1])
        row_ends = sb("row_ends", [1, 2 * P])
        row_counts = sb("row_counts", [1, P + 1])
        carry = sb("carry", [P, 1])
        inverse = sb("inverse", [P, COLS])
        pair_idx = sb("pair_idx", [P, GROUPS, TILES], I32)
        row_idx = sb("row_idx", [P, GROUPS, TILES], I32)
        g_idx = sb("g_idx", [P, GROUPS, TILES], I32)
        dst_idx = sb("dst_idx", [P, GROUPS, TILES], I32)
        node_at = sb("node_at", [P, GROUPS, TILES])
        twin_at = sb("twin_at", [P, GROUPS, TILES])
        w1 = sb("w1", [3 * EFEAT, HID])
        w1_u = sb("w1_u", [HID, 1])
        b1_c = sb("b1_c", [HID, 1])
        u0 = sb("u0", [P, 1])
        c1 = sb("c1", [HID, 1])
        c1_relu = sb("c1_relu", [HID, P])
        w2 = sb("w2", [HID, FEAT])
        b2_b = sb("b2_b", [P, FEAT])
        w_in = sb("w_in", [FEAT, FEAT])
        w_t = sb("w_t", [FEAT, FEAT])
        b_b = sb("b_b", [P, FEAT])
        eps = sb("eps", [P, 1])
        c0_tile = sb("c0_tile", [P, TROWS, FEAT])
        g0_tile = sb("g0_tile", [P, TROWS, FEAT])
        g0_relu = sb("g0_relu", [P, FEAT])
        g0_sum = sb("g0_sum", [P, 1])
        g0_row = sb("g0_row", [P, FEAT])
        idx_in = [sb(f"idx_in{n}", [P, TILES], I32) for n in range(PER)]
        idx_out = [sb(f"idx_out{n}", [P, TILES], I32) for n in range(PER)]
        pairs = [sb(f"pairs{n}", [P, TILES, PAIR_ROW]) for n in range(PER)]
        wrong = [sb(f"wrong{n}", [P, TILES]) for n in range(PER)]
        odd = [sb(f"odd{n}", [P, TILES], I32) for n in range(PER)]
        same_b = [sb(f"same_b{n}", [FEAT, COLS]) for n in range(PER)]
        floor_b = [sb(f"floor_b{n}", [EFEAT, COLS]) for n in range(PER)]
        feats = [sb(f"feats{n}", [3 * EFEAT, COLS]) for n in range(PER)]
        inverse_b = [sb(f"inverse_b{n}", [EFEAT, COLS]) for n in range(PER)]
        hidden = [sb(f"hidden{n}", [HID, COLS]) for n in range(PER)]
        delta = [sb(f"delta{n}", [P, TILES, FEAT]) for n in range(PER)]
        near = sb("near", [P, LN_ROWS, 2, FEAT])
        y = sb("y", [P, LN_ROWS, FEAT])
        yc = sb("yc", [P, LN_ROWS, FEAT])
        ysq = sb("ysq", [P, LN_ROWS, FEAT])
        x1 = sb("x1", [P, LN_ROWS, FEAT])
        ysum = sb("ysum", [P, LN_ROWS])
        ymean = sb("ymean", [P, LN_ROWS])
        yvar = sb("yvar", [P, LN_ROWS])
        ystd = sb("ystd", [P, LN_ROWS])
        yrstd = sb("yrstd", [P, LN_ROWS])
        aggr = [sb(f"aggr{n}", [FEAT, COLS]) for n in range(PER)]
        gz = sb("gz", [P, STEP_CHUNKS, FEAT])
        gr = sb("gr", [P, STEP_CHUNKS, FEAT])
        gsum = sb("gsum", [P, STEP_CHUNKS])
        gmean = sb("gmean", [P, STEP_CHUNKS])
        spare = pair_tile[:].rearrange("p q t w -> p (q t w)")

        def carve(k):
            return spare[:, k * TROWS * FEAT:(k + 1) * TROWS * FEAT].rearrange("p (c f) -> p c f", f=FEAT)

        in_x1, in_g, z, zsq, z_out = ([carve(2 * k), carve(2 * k + 1)] for k in range(5))
        zvar = [sb(f"zvar{n}", [P, TROWS]) for n in range(2)]
        zstd = [sb(f"zstd{n}", [P, TROWS]) for n in range(2)]
        zrstd = [sb(f"zrstd{n}", [P, TROWS]) for n in range(2)]

        p_turn = [ps(f"p_turn{n}", [P, COLS]) for n in range(2)]
        p_feat = [ps(f"p_feat{n}", [FEAT, COLS]) for n in range(PER)]
        p_hid = [ps(f"p_hid{n}", [HID, COLS]) for n in range(PER)]
        p_rows_banks = ps("p_rows", [P, PER * COLS])
        p_rows = p_rows_banks[:].rearrange("p (n t f) -> p n t f", n=PER, f=FEAT)[:, :, 0:TILES, :]

        pool_stands, pe_stands, dve_stands = sem("pool_stands"), sem("pe_stands"), sem("dve_stands")
        src_in, dst_in, attr_in = sem("src_in"), sem("dst_in"), sem("attr_in")
        weights_in = sem("weights_in")
        ident_zero, ident_done = sem("ident_zero"), sem("ident_done")
        pair_iota, part_iota = sem("pair_iota"), sem("part_iota")
        setup = sem("setup")
        w_turned, w_t_ready = sem("w_turned"), sem("w_t_ready")
        c1_ready, c1_relu_ready = sem("c1_ready"), sem("c1_relu_ready")
        c0_psum, c0_ready, g0_ready = sem("c0_psum"), sem("c0_ready"), sem("g0_ready")
        g0_relu_done = sem("g0_relu_done")
        pair_ids, pairs_out = sem("pair_ids"), sem("pairs_out")
        sorting = sem("sorting")
        turn_ready, sort_done = sem("turn_ready"), sem("sort_done")
        turned, untangled = sem("turned"), sem("untangled")
        words_out, near_words, flags_out = sem("words_out"), sem("near_words"), sem("flags_out")
        idx_turned, idx_kept = sem("idx_turned"), sem("idx_kept")
        pairs_known = sem("pairs_known")
        counts_local, counts_turned, rows_counted, carry_turned, inverse_ready = (
            sem("counts_local"), sem("counts_turned"), sem("rows_counted"), sem("carry_turned"), sem("inverse_ready"))
        tables = sem("tables")
        c0_out = [sem(f"c0_out{n}") for n in range(2)]
        g0_out, x_out = sem("g0_out"), [sem(f"x_out{n}") for n in range(2)]
        in_idx = [sem(f"in_idx{n}") for n in range(PER)]
        out_idx = [sem(f"out_idx{n}") for n in range(PER)]
        gathered = [sem(f"gathered{n}") for n in range(PER)]
        scattered = [sem(f"scattered{n}") for n in range(PER)]
        flags_in = [sem(f"flags_in{n}") for n in range(PER)]
        edge_known, edge_odd, edge_picked = sem("edge_known"), sem("edge_odd"), sem("edge_picked")
        dst_kept = sem("dst_kept")
        attrs_turned = sem("attrs_turned")
        summed, maxed, averaged = sem("summed"), sem("maxed"), sem("averaged")
        hid_psum, hid_ready, delta_psum, delta_ready = sem("hid_psum"), sem("hid_ready"), sem("delta_psum"), sem("delta_ready")
        g_idx_ready = sem("g_idx_ready")
        l1_in_idx = [sem(f"l1_in_idx{n}") for n in range(PER)]
        l1_out_idx = [sem(f"l1_out_idx{n}") for n in range(PER)]
        l1_gathered, l1_scattered = sem("l1_gathered"), sem("l1_scattered")
        l1_flags_in = [sem(f"l1_flags_in{n}") for n in range(PER)]
        tile_in = sem("tile_in")
        y_ready, ysum_ready, ymean_ready, yc_ready = sem("y_ready"), sem("ysum_ready"), sem("ymean_ready"), sem("yc_ready")
        ysq_ready, yvar_ready, ystd_ready, yrstd_ready = sem("ysq_ready"), sem("yvar_ready"), sem("ystd_ready"), sem("yrstd_ready")
        x1_ready, x1_out = sem("x1_ready"), sem("x1_out")
        x1_turned, aggr_ready, g_psum = sem("x1_turned"), sem("aggr_ready"), sem("g_psum")
        gz_ready, gr_ready, gsum_ready, gmean_ready, g_ready = sem("gz_ready"), sem("gr_ready"), sem("gsum_ready"), sem("gmean_ready"), sem("g_ready")
        z_in = [sem(f"z_in{n}") for n in range(2)]
        z_added, z_squared, zvar_ready, zstd_ready, zrstd_ready, z_done = sem("z_added"), sem("z_squared"), sem("zvar_ready"), sem("zstd_ready"), sem("zrstd_ready"), sem("z_done")
        out_done = [sem(f"out_done{n}") for n in range(2)]

        block = ctx.enter_context(nc.Block())

        def group_of(s, n):
            g = s * PER + n
            return bass.ds(g, 1) if not isinstance(g, int) else slice(g, g + 1)

        def tile_rows(t, parts=P):
            r = t * TILE
            return slice(r, r + parts * TROWS) if isinstance(t, int) else bass.ds(r, parts * TROWS)

        @block.sync
        def _(sp):
            sp.dma_start(src_i[0:EDGE_PARTS, :], src.rearrange("(p c) -> p c", p=EDGE_PARTS)).then_inc(src_in, 16)
            sp.dma_start(w1_u[:], W1[3 * EFEAT, :].rearrange("(h a) -> h a", a=1)).then_inc(weights_in, 16)
            sp.dma_start(b1_c[:], b1.rearrange("(h a) -> h a", a=1)).then_inc(weights_in, 16)
            sp.dma_start(u0[:], u[0, :].partition_broadcast(P)).then_inc(weights_in, 16)
            sp.dma_start(w2[:], W2).then_inc(weights_in, 16)
            sp.dma_start(b2_b[:], b2.partition_broadcast(P)).then_inc(weights_in, 16)
            sp.dma_start(b_b[:], b.partition_broadcast(P)).then_inc(weights_in, 16)
            sp.dma_start(w1[:], W1[0:3 * EFEAT, :]).then_inc(weights_in, 16)
            sp.dma_start(w_in[:], W).then_inc(weights_in, 16)
            sp.dma_start(dst_i[0:EDGE_PARTS, :], dst.rearrange("(p c) -> p c", p=EDGE_PARTS)).then_inc(dst_in, 16)
            attr_v = edge_attr.rearrange("(p q t) f -> p q t f", p=EDGE_PARTS, t=2)
            for t in range(2):
                sp.dma_start(pair_tile[0:EDGE_PARTS, :, t, 0:EFEAT], attr_v[:, :, t, :]).then_inc(attr_in, 16)
            sp.wait_ge(attr_in, 32)
            sp.wait_ge(pair_ids, 2)
            sp.dma_start(edge_pairs.rearrange("(p q) w -> p q w", p=EDGE_PARTS),
                         pair_tile[0:EDGE_PARTS].rearrange("p q t w -> p q (t w)")).then_inc(pairs_out, 16)

            def first_delta(t, n):
                sp.dma_start(node_rows[tile_rows(t), 1, :].rearrange("(p c) f -> p c f", p=P),
                             c0_tile[:]).then_inc(c0_out[n], 16)

            sp.wait_ge(c0_ready, 1)
            first_delta(0, 0)
            first_delta(1, 1)
            with sp.Fori(1, C0_EARLY // 2) as i:
                for n in range(2):
                    sp.wait_ge(c0_out[n], i * 16)
                    first_delta(i * 2 + n, n)
            for t in range(C0_EARLY // 2 * 2, STEPS):
                sp.wait_ge(c0_out[t % 2], t // 2 * 16)
                first_delta(t, t % 2)

            def load_flags(target, row, s, n, ready):
                at = (s * PER + n) * COLS
                cols = slice(at, at + COLS) if isinstance(at, int) else bass.ds(at, COLS)
                sp.dma_start(target, flags[row, cols].partition_broadcast(target.shape[0])).then_inc(ready[n], 16)

            def load_idx(slot, table, s, n, ready):
                sp.dma_start(slot[n][:], table[:, group_of(s, n), :].rearrange("p a t -> p (a t)")).then_inc(ready[n], 16)

            def l0_step(s, first=False):
                if not isinstance(s, int) or s < STEPS:
                    for n in range(PER):
                        if not first:
                            sp.wait_ge(gathered[n], s * 16 * TILES)
                        load_idx(idx_in, pair_idx, s, n, in_idx)
                if not first:
                    for n in range(PER):
                        if isinstance(s, int) and s == 1:
                            sp.wait_ge(idx_kept, 4)
                        else:
                            sp.wait_ge(scattered[n], (s - 1) * 16 * TILES)
                        load_idx(idx_out, row_idx, s - 1, n, out_idx)
                if not isinstance(s, int) or s < STEPS:
                    for n in range(PER):
                        if not first:
                            sp.wait_ge(summed, (s - 1) * PER + n + 1)
                            sp.wait_ge(maxed, (s - 1) * PER + n + 1)
                            sp.wait_ge(averaged, (s - 1) * PER + n + 1)
                        else:
                            sp.wait_ge(flags_out, 48)
                        load_flags(same_b[n][0:EFEAT, :], 0, s, n, flags_in)
                        load_flags(floor_b[n][:], 1, s, n, flags_in)
                        load_flags(inverse_b[n][:], 2, s, n, flags_in)
                    rows = tile_rows(s, P)
                    if isinstance(s, int) and s == STEPS - 1:
                        rows = tile_rows(s, LAST_PARTS)
                    sp.dma_start(node_rows[rows, 0, :], x[rows, :]).then_inc(x_out[0], 16)

            sp.wait_ge(idx_kept, 1)
            l0_step(0, first=True)
            l0_step(1)
            with sp.Fori(2, STEPS - 1) as s:
                l0_step(s)
            l0_step(STEPS - 1)
            l0_step(STEPS)
            sp.dma_start(node_rows[NODES:N_PAD, 0, :], x[0:N_PAD - NODES, :]).then_inc(x_out[1], 16)

            sp.wait_ge(g_idx_ready, 1)
            sp.wait_ge(dst_kept, GROUPS)
            sp.wait_ge(x_out[0], 16 * STEPS)
            sp.wait_ge(x_out[1], 16)
            for n in range(PER):
                sp.wait_ge(scattered[n], 16 * TILES * STEPS)

            def l1_load(s):
                if not (isinstance(s, int) and s == 0):
                    sp.wait_ge(l1_gathered, s * 16 * STEP_CHUNKS)
                for n in range(PER):
                    load_idx(idx_in, dst_idx, s, n, l1_in_idx)
                if not (isinstance(s, int) and s == 0):
                    sp.wait_ge(y_ready, s)
                sp.dma_start(near[:, STEP_CHUNKS:, :, :],
                             node_rows[tile_rows(s)].rearrange("(p c) t f -> p c t f", p=P)).then_inc(tile_in, 16)

            def l1_keep(s):
                sp.wait_ge(x1_ready, (s + 1) * 2)
                sp.dma_start(x1_table[tile_rows(s), :].rearrange("(p c) f -> p c f", p=P),
                             x1[:, STEP_CHUNKS:, :]).then_inc(x1_out, 16)

            def l1_flags(s):
                for n in range(PER):
                    if not (isinstance(s, int) and s == 0):
                        sp.wait_ge(aggr_ready, (s - 1) * PER + n + 1)
                    load_flags(same_b[n][:], 0, s, n, l1_flags_in)

            def l1_out(s):
                if not (isinstance(s, int) and s == 0):
                    sp.wait_ge(l1_scattered, s * 16 * STEP_CHUNKS)
                for n in range(PER):
                    load_idx(idx_out, g_idx, s, n, l1_out_idx)

            sp.wait_ge(averaged, GROUPS)
            l1_load(0)
            l1_flags(0)
            l1_out(0)
            l1_load(1)
            l1_keep(0)
            l1_flags(1)
            l1_load(2)
            l1_keep(1)
            l1_flags(2)
            with sp.Fori(2, STEPS - 1) as s:
                l1_load(s + 1)
                l1_keep(s)
                l1_flags(s + 1)
                l1_out(s - 1)
            l1_keep(STEPS - 1)
            l1_out(STEPS - 2)
            l1_out(STEPS - 1)

            sp.wait_ge(l1_scattered, 16 * STEP_CHUNKS * STEPS)
            sp.wait_ge(x1_out, 16 * STEPS)

            def load_tile(t, n):
                sp.dma_start(in_x1[n], x1_table[tile_rows(t), :].rearrange("(p c) f -> p c f", p=P)).then_inc(z_in[n], 16)
                sp.dma_start(in_g[n], g_table[tile_rows(t), :].rearrange("(p c) f -> p c f", p=P)).then_inc(z_in[n], 16)

            load_tile(0, 0)
            load_tile(1, 1)
            with sp.Fori(1, STEPS // 2) as i:
                for n in range(2):
                    sp.wait_ge(z_added, (i - 1) * 2 + n + 1)
                    load_tile(i * 2 + n, n)
            sp.wait_ge(z_added, STEPS - 2)
            load_tile(STEPS - 1, 0)

        @block.gpsimd
        def _(pool):
            pool.iota(pair_i[:], pattern=[[1, PAIR_COLS], [0, 2]], base=0,
                      channel_multiplier=PAIR_COLS).then_inc(pair_iota, 1)
            pool.iota(part_i[:], pattern=[[0, 1]], base=0, channel_multiplier=1).then_inc(part_iota, 1)
            pool.memset(ident[:], 0.0).then_inc(ident_zero, 1)
            pool.wait_ge(ident_zero, 1)
            pool.affine_select(out=ident[:], in_=ident[:], compare_op=ALU.not_equal, fill=1.0, base=0,
                               pattern=[[-1, P]], channel_multiplier=1).then_inc(ident_done, 1)

            def gather(n, target, table, top, ready):
                pool.sem_inc(pool_stands, 1)
                for t in range(TILES):
                    pool.indirect_dma_start(out=target(t), out_offset=None, in_=table,
                                            in_offset=bass.IndirectOffsetOnAxis(ap=idx_in[n][:, t:t + 1], axis=0),
                                            bounds_check=top, oob_is_err=False).then_inc(ready, 16)

            def scatter(n, source, table, top, ready):
                pool.sem_inc(pool_stands, 1)
                for t in range(TILES):
                    pool.indirect_dma_start(out=table, in_=source(t), in_offset=None,
                                            out_offset=bass.IndirectOffsetOnAxis(ap=idx_out[n][:, t:t + 1], axis=0),
                                            bounds_check=top, oob_is_err=False).then_inc(ready, 16)

            def l0_gather(s, first=False):
                for n in range(PER):
                    pool.wait_ge(in_idx[n], (s + 1) * 16)
                    if not first:
                        pool.wait_ge(attrs_turned, (s - 1) * PER + n + 1)
                        pool.wait_ge(dst_kept, (s - 1) * PER + n + 1)
                    gather(n, lambda t, n=n: pairs[n][:, t, :], edge_pairs, EDGES // 2 - 1, gathered[n])

            def l0_scatter(s):
                for n in range(PER):
                    pool.wait_ge(out_idx[n], (s + 1) * 16)
                    pool.wait_ge(delta_ready, s * PER + n + 1)
                    scatter(n, lambda t, n=n: delta[n][:, t, :], node_halves, 2 * N_PAD - 1, scattered[n])

            pool.wait_ge(pairs_out, 16)
            l0_gather(0, first=True)
            l0_gather(1)
            for n in range(2):
                pool.wait_ge(c0_out[n], 16 * ((STEPS + 1 - n) // 2))
            l0_scatter(0)
            with pool.Fori(2, STEPS) as s:
                l0_gather(s)
                l0_scatter(s - 1)
            l0_scatter(STEPS - 1)

            for n in range(PER):
                pool.wait_ge(scattered[n], 16 * TILES * STEPS)
            pool.wait_ge(x_out[0], 16 * STEPS)

            def l1_gather(s, first=False):
                if not first:
                    pool.wait_ge(y_ready, s)
                for n in range(PER):
                    pool.wait_ge(l1_in_idx[n], (s + 1) * 16)
                    gather(n, lambda t, n=n: near[:, n * TILES + t, :, :].rearrange("p t f -> p (t f)"),
                           node_pairs, N_PAD - 1, l1_gathered)

            def l1_scatter(s):
                pool.wait_ge(g_ready, s + 1)
                for n in range(PER):
                    pool.wait_ge(l1_out_idx[n], (s + 1) * 16)
                    scatter(n, lambda t, n=n: delta[n][:, t, :], g_table, N_PAD - 1, l1_scattered)

            l1_gather(0, first=True)
            l1_gather(1)
            pool.wait_ge(g0_out, 16 * STEPS)
            with pool.Fori(2, STEPS) as s:
                l1_gather(s)
                l1_scatter(s - 2)
            l1_scatter(STEPS - 2)
            l1_scatter(STEPS - 1)

        @block.scalar
        def _(act):
            act.wait_ge(weights_in, 16 * 8)
            act.activation(g0_relu[:], b_b[:], ACT.Relu).then_inc(g0_relu_done, 1)

            act.wait_ge(attr_in, 32)
            act.wait_ge(dst_in, 16)
            act.activation(pair_tile[0:EDGE_PARTS, :, :, EFEAT],
                           dst_i[0:EDGE_PARTS, :].rearrange("p (q t) -> p q t", t=2), ACT.Copy).then_inc(pair_ids, 1)
            act.wait_ge(src_in, 16)
            act.activation(pair_tile[0:EDGE_PARTS, :, :, EFEAT + 1],
                           src_i[0:EDGE_PARTS, :].rearrange("p (q t) -> p q t", t=2), ACT.Copy).then_inc(pair_ids, 1)

            for n in range(2 * (LEVELS - ROW_LEVELS)):
                act.wait_ge(turned, n + 1)
                to = KT[0] if n % 2 == 0 else K[0]
                act.activation(to[:], p_turn[n % 2][:], ACT.Copy).then_inc(untangled, 1)

            act.wait_ge(setup, 2)
            act.dma_start(words[0:1].rearrange("(a c) -> a c", a=1), sentinel[:]).then_inc(words_out, 16)
            act.dma_start(words[P * COLS + 1:P * COLS + 2].rearrange("(a c) -> a c", a=1), sentinel[:]).then_inc(words_out, 16)
            act.wait_ge(sort_done, 1)
            act.dma_start(words[1:P * COLS + 1].rearrange("(p c) -> p c", p=P), K[1][:]).then_inc(words_out, 16)
            act.wait_ge(words_out, 48)
            act.dma_start(prev[:], words[0:P * COLS].rearrange("(p c) -> p c", p=P)).then_inc(near_words, 16)
            act.dma_start(nxt[:], words[2:P * COLS + 2].rearrange("(p c) -> p c", p=P)).then_inc(near_words, 16)
            def keep_table(n, to):
                act.wait_ge(idx_turned, n + 1)
                turned_v = p_turn[n % 2][:].rearrange("p (t g) -> p g t", t=TILES)
                act.activation(to[:], turned_v[:, 0:GROUPS, :], ACT.Copy).then_inc(idx_kept, 1)

            keep_table(0, pair_idx)
            act.wait_ge(tables, 1)
            act.dma_start(flags[0, :].rearrange("(p c) -> p c", p=P), same[:]).then_inc(flags_out, 16)
            act.dma_start(flags[1, :].rearrange("(p c) -> p c", p=P), floor_f[:]).then_inc(flags_out, 16)
            for n, to in enumerate((row_idx, node_at, twin_at)):
                keep_table(n + 1, to)
            act.wait_ge(inverse_ready, 1)
            act.dma_start(flags[2, :].rearrange("(p c) -> p c", p=P), inverse[:]).then_inc(flags_out, 16)

            def l0_hidden(s, first=False):
                for n in range(PER):
                    act.wait_ge(hid_psum, s * PER + n + 1)
                    if not first:
                        act.wait_ge(delta_psum, (s - 1) * PER + n + 1)
                    act.activation(hidden[n][:], p_hid[n][:], ACT.Relu, bias=c1[:, 0:1]).then_inc(hid_ready, 1)
                act.dma_start(g_table[tile_rows(s), :].rearrange("(p c) f -> p c f", p=P), g0_tile[:]).then_inc(g0_out, 16)

            act.wait_ge(g0_ready, 1)
            act.wait_ge(c1_ready, 1)
            l0_hidden(0, first=True)
            with act.Fori(1, STEPS) as s:
                l0_hidden(s)

            def l1_square(s):
                act.wait_ge(yc_ready, s + 1)
                act.activation(ysq[:], yc[:], ACT.Square).then_inc(ysq_ready, 1)

            def l1_deviation(s):
                act.wait_ge(yvar_ready, s + 1)
                act.activation(ystd[:], yvar[:], ACT.Sqrt, bias=eps[:, 0:1], scale=1.0 / FEAT).then_inc(ystd_ready, 1)

            l1_square(0)
            l1_deviation(0)
            with act.Fori(1, STEPS) as s:
                l1_square(s)
                act.wait_ge(gz_ready, s)
                act.activation(gr[:], gz[:], ACT.Relu).then_inc(gr_ready, 1)
                l1_deviation(s)
            act.wait_ge(gz_ready, STEPS)
            act.activation(gr[:], gz[:], ACT.Relu).then_inc(gr_ready, 1)

            def square(t, n):
                act.wait_ge(z_added, t + 1)
                act.activation(zsq[n], z[n], ACT.Square).then_inc(z_squared, 1)

            def deviation(t, n):
                act.wait_ge(zvar_ready, t + 1)
                act.activation(zstd[n][:], zvar[n][:], ACT.Sqrt, bias=eps[:, 0:1], scale=1.0 / FEAT).then_inc(zstd_ready, 1)

            def store(t, n, parts=P):
                act.wait_ge(z_done, t + 1)
                act.dma_start(out[tile_rows(t, parts), :].rearrange("(p c) f -> p c f", p=parts),
                              z_out[n][0:parts]).then_inc(out_done[n], 16)

            square(0, 0)
            square(1, 1)
            deviation(0, 0)
            with act.Fori(1, STEPS // 2) as i:
                for n in range(2):
                    square(i * 2 + n, n)
                    deviation(i * 2 + n - 1, 1 - n)
                    store(i * 2 + n - 2, n)
            t = STEPS - 1
            square(t, 0)
            deviation(t - 1, 1)
            store(t - 2, 0)
            deviation(t, 0)
            store(t - 1, 1)
            store(t, 0, LAST_PARTS)
            act.wait_ge(out_done[0], 16 * (STEPS // 2 + 1))
            act.wait_ge(out_done[1], 16 * (STEPS // 2))

        @block.tensor
        def _(pe):
            pe.wait_ge(c1_relu_ready, 1)
            pe.matmul(p_rows[:, 0, 0, :], c1_relu[:], w2[:], start=True, stop=True).then_inc(c0_psum, 1)
            pe.wait_ge(ident_done, 1)
            pe.wait_ge(weights_in, 16 * 8)
            pe.transpose(p_hid[0][0:FEAT, 0:FEAT], w_in[:], ident[0:FEAT, 0:FEAT]).then_inc(w_turned, 1)
            for n in range(2 * (LEVELS - ROW_LEVELS)):
                pe.wait_ge(turn_ready, n + 1)
                if n % 2:
                    from_ = KT[(n // 2 + 1) % 2]
                else:
                    from_ = K[1 if n == 0 else 0]
                for t in range(TILES):
                    ins = pe.transpose(p_turn[n % 2][:, t * P:(t + 1) * P], from_[:, t * P:(t + 1) * P], ident[:])
                ins.then_inc(turned, 1)
            for n, from_ in enumerate((pair_f, row_f, node, twin)):
                if n == 0:
                    pe.wait_ge(pairs_known, 1)
                else:
                    pe.wait_ge(tables, 1)
                if n >= 2:
                    pe.wait_ge(idx_kept, n - 1)
                for t in range(TILES):
                    ins = pe.transpose(p_turn[n % 2][:, t * P:(t + 1) * P], from_[:, t * P:(t + 1) * P], ident[:])
                ins.then_inc(idx_turned, 1)

            pe.wait_ge(counts_local, 1)
            pe.transpose(p_hid[1][0:1, 0:P], count[:, COLS - 1:COLS], ident[:])
            pe.transpose(p_hid[1][0:1, P:2 * P], whole[:], ident[:]).then_inc(counts_turned, 1)
            pe.wait_ge(rows_counted, 1)
            pe.transpose(p_hid[1][:, 2 * P:2 * P + 1], row_counts[0:1, 0:P], ident[0:1, 0:1]).then_inc(carry_turned, 1)

            def l0_turn(s, n, first=False):
                pe.wait_ge(edge_picked, s * PER + n + 1)
                if not first:
                    pe.wait_ge(maxed, (s - 1) * PER + n + 1)
                for t in range(TILES):
                    ins = pe.transpose(p_feat[n][0:EFEAT, t * P:(t + 1) * P], pairs[n][:, t, 0:EFEAT], ident[:])
                ins.then_inc(attrs_turned, 1)

            def l0_mlp_in(s, n, first=False):
                pe.wait_ge(averaged, s * PER + n + 1)
                if not first:
                    pe.wait_ge(hid_ready, (s - 1) * PER + n + 1)
                pe.matmul(p_hid[n][:], w1[:], feats[n][:], start=True, stop=True).then_inc(hid_psum, 1)

            def l0_mlp_out(s, n, first=False):
                pe.wait_ge(hid_ready, s * PER + n + 1)
                if not first:
                    pe.wait_ge(delta_ready, (s - 1) * PER + n + 1)
                for t in range(TILES):
                    ins = pe.matmul(p_rows[:, n, t, :], hidden[n][:, t * P:(t + 1) * P], w2[:],
                                    start=True, stop=True)
                ins.then_inc(delta_psum, 1)

            def l0_pe(s, first=False):
                l0_turn(s, 0, first)
                l0_mlp_in(s, 0, first)
                l0_turn(s, 1, first)
                l0_mlp_out(s, 0, first)
                l0_mlp_in(s, 1, first)
                l0_mlp_out(s, 1, first)

            pe.wait_ge(weights_in, 16 * 8)
            pe.wait_ge(c0_ready, 1)
            pe.wait_ge(w_t_ready, 1)
            l0_pe(0, first=True)
            with pe.Fori(1, STEPS) as s:
                l0_pe(s)

            def l1_pe(s, first=False):
                pe.wait_ge(x1_ready, s * 2 + 1)
                for n in range(PER):
                    if not first:
                        pe.wait_ge(aggr_ready, (s - 1) * PER + n + 1)
                    pe.sem_inc(pe_stands, 1)
                    for t in range(TILES):
                        ins = pe.transpose(p_feat[n][:, t * P:(t + 1) * P], x1[:, n * TILES + t, :], ident[:])
                    ins.then_inc(x1_turned, 1)
                for n in range(PER):
                    pe.wait_ge(aggr_ready, s * PER + n + 1)
                    if not first and n == 0:
                        pe.wait_ge(gz_ready, s)
                    for t in range(TILES):
                        ins = pe.matmul(p_rows[:, n, t, :], aggr[n][:, t * P:(t + 1) * P], w_t[:],
                                        start=True, stop=True)
                    ins.then_inc(g_psum, 1)

            pe.wait_ge(delta_ready, GROUPS)
            l1_pe(0, first=True)
            with pe.Fori(1, STEPS) as s:
                l1_pe(s)

        @block.vector
        def _(dve):
            steps = [0]

            def link(ins):
                steps[0] += 1
                ins.then_inc(sorting, 1)
                dve.wait_ge(sorting, steps[0])

            def mark(ins):
                steps[0] += 1
                ins.then_inc(sorting, 1)

            mark(dve.memset(one[:], 1.0))
            mark(dve.memset(row_counts[:, 0:1], 0.0))
            mark(dve.memset(feats[1][:, COLS - 1:COLS], 0.0))
            mark(dve.memset(aggr[1][:, COLS - 1:COLS], 0.0))
            dve.memset(eps[:], EPS).then_inc(setup, 1)
            dve.memset(sentinel[:], PAD).then_inc(setup, 1)
            link(dve.memset(K[0][:], PAD))
            q = slice(0, EDGE_PARTS)
            dve.wait_ge(src_in, 16)
            link(dve.tensor_copy(src_f[q, :], src_i[q, :]))
            link(dve.tensor_scalar(high[q, :], src_f[q, :], float(HALF), float(SIGN_CODE - HALF), ALU.is_ge, ALU.mult))
            link(dve.scalar_tensor_tensor(out=code_i[q, :], in0=src_f[q, :], scalar=float(CODE0), in1=high[q, :],
                                          op0=ALU.add, op1=ALU.add))
            link(dve.tensor_scalar(code_s[q, :], code_i[q, :], PAIR_BITS, None, ALU.logical_shift_left))
            dve.wait_ge(pair_iota, 1)
            link(dve.tensor_tensor(K[0][q, 0:EDGE_COLS].bitcast(I32), code_s[q, :], pair_i[q, :], ALU.bitwise_or))
            dve.wait_ge(weights_in, 16 * 8)
            dve.tensor_scalar(c1[:], w1_u[:], u0[:, 0:1], b1_c[:, 0:1], ALU.mult, ALU.add).then_inc(c1_ready, 1)
            dve.wait_ge(c1_ready, 1)
            dve.tensor_scalar(c1_relu[:], c1[:, 0:1].broadcast_to([HID, P]), 0.0, None, ALU.max).then_inc(c1_relu_ready, 1)
            dve.wait_ge(g0_relu_done, 1)
            link(dve.tensor_reduce(g0_sum[:], g0_relu[:], AX_X, ALU.add))
            link(dve.tensor_scalar(g0_sum[:], g0_sum[:], 1.0 / FEAT, None, ALU.mult))
            link(dve.tensor_scalar(g0_row[:], g0_relu[:], g0_sum[:, 0:1], None, ALU.subtract))
            dve.tensor_copy(g0_tile[:], g0_row[:].unsqueeze(1).broadcast_to([P, TROWS, FEAT])).then_inc(g0_ready, 1)
            dve.wait_ge(c0_psum, 1)
            dve.tensor_tensor(c0_tile[:], p_rows[:, 0, 0:1, :].broadcast_to([P, TROWS, FEAT]),
                              b2_b[:].unsqueeze(1).broadcast_to([P, TROWS, FEAT]), ALU.add).then_inc(c0_ready, 1)
            dve.wait_ge(w_turned, 1)
            dve.tensor_copy(w_t[:], p_hid[0][0:FEAT, 0:FEAT]).then_inc(w_t_ready, 1)
            dve.wait_ge(part_iota, 1)
            for bit in range(8):
                mark(dve.tensor_scalar(bit_a[:, bit:bit + 1], part_i[:], bit, None, ALU.logical_shift_right))
            dve.wait_ge(sorting, steps[0])
            link(dve.tensor_scalar(bit_b[:], bit_a[:], 1, None, ALU.bitwise_and))
            link(dve.tensor_scalar(sign[:], bit_b[:], -2.0, 1.0, ALU.mult, ALU.add))
            link(dve.tensor_tensor(flip[:, 0:7], sign[:, 0:7], sign[:, 1:8], ALU.mult))
            link(dve.tensor_scalar(K[1][:], K[0][:], sign[:, 0:1], None, ALU.mult))

            def exchange(bufs, cur, dist, mirrored=False, ends_phase=None):
                a = bufs[cur][:].rearrange("p (a t d) -> p a t d", t=2, d=dist)
                o = bufs[1 - cur][:].rearrange("p (a t d) -> p a t d", t=2, d=dist)
                left, right = a[:, :, 0, :], a[:, :, 1, :]
                back = slice(None, None, -1) if mirrored and dist > 1 else slice(None)
                dve.tensor_tensor(o[:, :, 0, :], left, right[:, :, back], ALU.min)
                ins = dve.tensor_tensor(o[:, :, 1, :], right, left[:, :, back], ALU.max)
                if ends_phase is not None:
                    ins.then_inc(ends_phase, 1)
                else:
                    link(ins)
                return 1 - cur

            cur = 1
            for level in range(1, ROW_LEVELS + 1):
                cur = exchange(K, cur, 2 ** (level - 1), mirrored=True)
                for d in range(level - 2, -1, -1):
                    cur = exchange(K, cur, 2 ** d)
            for level in range(ROW_LEVELS + 1, LEVELS + 1):
                m = level - ROW_LEVELS - 1
                dve.tensor_scalar(K[1 - cur][:], K[cur][:], flip[:, m:m + 1], None, ALU.mult).then_inc(turn_ready, 1)
                dve.wait_ge(untangled, 2 * m + 1)
                cur = 0
                for d in range(m, -1, -1):
                    cur = exchange(KT, cur, 2 ** d, ends_phase=turn_ready if d == 0 else None)
                dve.wait_ge(untangled, 2 * m + 2)
                cur = 0
                for d in range(ROW_LEVELS - 1, -1, -1):
                    cur = exchange(K, cur, 2 ** d, ends_phase=sort_done if d == 0 and level == LEVELS else None)
            dve.wait_ge(sort_done, 1)

            here = K[1]
            link(dve.tensor_scalar(code_here[:], here[:].bitcast(I32), PAIR_BITS, None, ALU.logical_shift_right))
            link(dve.tensor_scalar(pair_bits[:], here[:].bitcast(I32), 2 ** PAIR_BITS - 1, None, ALU.bitwise_and))
            dve.tensor_copy(pair_f[:], pair_bits[:]).then_inc(pairs_known, 1)
            link(dve.tensor_scalar(upper[:], code_here[:], float(SIGN_CODE), float(HALF - SIGN_CODE), ALU.is_ge, ALU.mult))
            link(dve.scalar_tensor_tensor(out=node[:], in0=code_here[:], scalar=float(-CODE0), in1=upper[:],
                                          op0=ALU.add, op1=ALU.add))
            dve.wait_ge(near_words, 32)
            mark(dve.tensor_scalar(code_prev[:], prev[:].bitcast(I32), PAIR_BITS, None, ALU.logical_shift_right))
            link(dve.tensor_scalar(code_next[:], nxt[:].bitcast(I32), PAIR_BITS, None, ALU.logical_shift_right))
            mark(dve.tensor_tensor(same[:], code_here[:], code_prev[:], ALU.is_equal))
            mark(dve.tensor_tensor(ends[:], code_here[:], code_next[:], ALU.is_equal))
            link(dve.tensor_tensor(twin[:], here[:], prev[:], ALU.is_equal))
            link(dve.tensor_scalar(floor_f[:], same[:], 2.0, -1.0, ALU.mult, ALU.add))
            link(dve.tensor_scalar(floor_f[:], floor_f[:], FLT_MAX, None, ALU.mult))
            link(dve.tensor_scalar(skip[:], ends[:], SKIP, 1.0, ALU.mult, ALU.add))
            dve.scalar_tensor_tensor(out=row_f[:], in0=node[:], scalar=2.0, in1=skip[:],
                                     op0=ALU.mult, op1=ALU.add).then_inc(tables, 1)

            ones = one[:, 0:1].broadcast_to([P, COLS])
            mark(dve.tensor_tensor_scan(count[:], same[:], ones, 0.0, ALU.mult, ALU.add))
            dve.tensor_reduce(whole[:], same[:], AX_X, ALU.min).then_inc(counts_local, 1)
            dve.wait_ge(counts_turned, 1)
            link(dve.tensor_copy(row_ends[:], p_hid[1][0:1, 0:2 * P]))
            dve.tensor_tensor_scan(row_counts[:, 1:P + 1], row_ends[:, P:2 * P], row_ends[:, 0:P], 0.0,
                                   ALU.mult, ALU.add).then_inc(rows_counted, 1)
            dve.wait_ge(carry_turned, 1)
            link(dve.tensor_copy(carry[:], p_hid[1][:, 2 * P:2 * P + 1]))
            link(dve.tensor_tensor_scan(count[:], same[:], ones, carry[:, 0:1], ALU.mult, ALU.add))
            dve.reciprocal(inverse[:], count[:]).then_inc(inverse_ready, 1)

            def l0_pick(s, n):
                g = s * PER + n
                at = group_of(s, n)
                dve.wait_ge(gathered[n], (s + 1) * 16 * TILES)
                dve.tensor_tensor(wrong[n][:], pairs[n][:, :, EFEAT + 1], node_at[:, at, :].rearrange("p a t -> p (a t)"),
                                  ALU.not_equal).then_inc(edge_known, 1)
                dve.wait_ge(edge_known, g + 1)
                dve.tensor_tensor(odd[n][:], wrong[n][:], twin_at[:, at, :].rearrange("p a t -> p (a t)"),
                                  ALU.max).then_inc(edge_odd, 1)
                dve.wait_ge(edge_odd, g + 1)
                dve.sem_inc(dve_stands, 1)
                dve.copy_predicated(out=pairs[n][:, :, 0:HALF_ROW], mask=odd[n][:].unsqueeze(2).broadcast_to([P, TILES, HALF_ROW]),
                                    data=pairs[n][:, :, HALF_ROW:PAIR_ROW]).then_inc(edge_picked, 1)
                dve.wait_ge(edge_picked, g + 1)
                dve.tensor_copy(dst_idx[:, at, :].rearrange("p a t -> p (a t)"), pairs[n][:, :, EFEAT]).then_inc(dst_kept, 1)

            def l0_scan(s, n, first=False):
                g = s * PER + n
                dve.wait_ge(attrs_turned, g + 1)
                dve.wait_ge(flags_in[n], (s + 1) * 48)
                if not first:
                    dve.wait_ge(hid_psum, (s - 1) * PER + n + 1)
                if not (first and n == 0):
                    dve.wait_ge(maxed, g)
                dve.tensor_tensor_scan(feats[n][0:EFEAT, :], same_b[n][0:EFEAT, :], p_feat[n][0:EFEAT, :],
                                       feats[1 - n][0:EFEAT, COLS - 1:COLS], ALU.mult, ALU.add).then_inc(summed, 1)
                dve.tensor_tensor_scan(feats[n][EFEAT:2 * EFEAT, :], floor_b[n][:], p_feat[n][0:EFEAT, :],
                                       feats[1 - n][EFEAT:2 * EFEAT, COLS - 1:COLS], ALU.min, ALU.max).then_inc(maxed, 1)
                dve.wait_ge(summed, g + 1)
                dve.tensor_tensor(feats[n][2 * EFEAT:3 * EFEAT, :], feats[n][0:EFEAT, :], inverse_b[n][:],
                                  ALU.mult).then_inc(averaged, 1)

            def l0_delta(s, n, first=False):
                dve.wait_ge(delta_psum, s * PER + n + 1)
                if not first:
                    dve.wait_ge(scattered[n], s * 16 * TILES)
                dve.tensor_tensor(delta[n][:], p_rows[:, n, :, :],
                                  b2_b[:].unsqueeze(1).broadcast_to([P, TILES, FEAT]), ALU.add).then_inc(delta_ready, 1)

            def l0_dve(s, first=False):
                for n in range(PER):
                    l0_pick(s, n)
                    l0_scan(s, n, first)
                for n in range(PER):
                    l0_delta(s, n, first)

            dve.wait_ge(idx_kept, 4)
            l0_dve(0, first=True)
            with dve.Fori(1, STEPS) as s:
                l0_dve(s)

            dve.tensor_scalar(g_idx[:], row_idx[:], -1.0, 0.5, ALU.add, ALU.mult).then_inc(g_idx_ready, 1)

            inv = 1.0 / FEAT

            def rows_b(a, rows=LN_ROWS):
                return a[:].unsqueeze(2).broadcast_to([P, rows, FEAT])

            def l1_norm(s, first=False):
                dve.wait_ge(l1_gathered, (s + 1) * 16 * STEP_CHUNKS)
                dve.wait_ge(tile_in, (s + 1) * 16)
                dve.tensor_tensor(y[:], near[:, :, 0, :], near[:, :, 1, :], ALU.add).then_inc(y_ready, 1)
                dve.wait_ge(y_ready, s + 1)
                dve.tensor_reduce(ysum[:], y[:], AX_X, ALU.add).then_inc(ysum_ready, 1)
                dve.wait_ge(ysum_ready, s + 1)
                dve.tensor_scalar(ymean[:], ysum[:], inv, None, ALU.mult).then_inc(ymean_ready, 1)
                dve.wait_ge(ymean_ready, s + 1)
                dve.tensor_tensor(yc[:], y[:], rows_b(ymean), ALU.subtract).then_inc(yc_ready, 1)

            def l1_scale(s, first=False):
                dve.wait_ge(ysq_ready, s + 1)
                dve.tensor_reduce(yvar[:], ysq[:], AX_X, ALU.add).then_inc(yvar_ready, 1)
                dve.wait_ge(ystd_ready, s + 1)
                dve.reciprocal(yrstd[:], ystd[:]).then_inc(yrstd_ready, 1)
                dve.wait_ge(yrstd_ready, s + 1)
                if not first:
                    dve.wait_ge(x1_turned, s * PER)
                    dve.wait_ge(x1_out, s * 16)
                for rows in (slice(0, STEP_CHUNKS), slice(STEP_CHUNKS, LN_ROWS)):
                    n_rows = rows.stop - rows.start
                    dve.tensor_tensor(x1[:, rows, :], yc[:, rows, :],
                                      yrstd[:, rows].unsqueeze(2).broadcast_to([P, n_rows, FEAT]), ALU.mult).then_inc(x1_ready, 1)

            def l1_sum(s, first=False):
                for n in range(PER):
                    g = s * PER + n
                    dve.wait_ge(x1_turned, g + 1)
                    dve.wait_ge(l1_flags_in[n], (s + 1) * 16)
                    if not first:
                        dve.wait_ge(g_psum, (s - 1) * PER + n + 1)
                    if not (first and n == 0):
                        dve.wait_ge(aggr_ready, g)
                    dve.tensor_tensor_scan(aggr[n][:], same_b[n][:], p_feat[n][:], aggr[1 - n][:, COLS - 1:COLS],
                                           ALU.mult, ALU.add).then_inc(aggr_ready, 1)

            def l1_bias(s):
                dve.wait_ge(g_psum, (s + 1) * PER)
                dve.tensor_tensor(gz[:].rearrange("p (n t) f -> p n t f", n=PER), p_rows,
                                  b_b[:].unsqueeze(1).unsqueeze(1).broadcast_to([P, PER, TILES, FEAT]),
                                  ALU.add).then_inc(gz_ready, 1)

            def l1_centre(s, first=False):
                dve.wait_ge(gr_ready, s + 1)
                dve.tensor_reduce(gsum[:], gr[:], AX_X, ALU.add).then_inc(gsum_ready, 1)
                dve.wait_ge(gsum_ready, s + 1)
                dve.tensor_scalar(gmean[:], gsum[:], inv, None, ALU.mult).then_inc(gmean_ready, 1)
                dve.wait_ge(gmean_ready, s + 1)
                if not first:
                    dve.wait_ge(l1_scattered, s * 16 * STEP_CHUNKS)
                for n in range(PER):
                    ins = dve.tensor_tensor(delta[n][:], gr[:, n * TILES:(n + 1) * TILES, :],
                                            gmean[:, n * TILES:(n + 1) * TILES].unsqueeze(2).broadcast_to([P, TILES, FEAT]),
                                            ALU.subtract)
                ins.then_inc(g_ready, 1)

            for n in range(PER):
                dve.wait_ge(scattered[n], 16 * TILES * STEPS)
            l1_norm(0)
            l1_scale(0, first=True)
            l1_sum(0, first=True)
            l1_norm(1)
            l1_bias(0)
            l1_scale(1)
            l1_sum(1)
            l1_centre(0, first=True)
            with dve.Fori(2, STEPS) as s:
                l1_norm(s)
                l1_bias(s - 1)
                l1_scale(s)
                l1_sum(s)
                l1_centre(s - 1)
            l1_bias(STEPS - 1)
            l1_centre(STEPS - 1)

            def add(t, n, first=False):
                dve.wait_ge(z_in[n], (t // 2 + 1) * 32 if isinstance(t, int) else (t + (2 - n)) * 16)
                dve.tensor_tensor(z[n], in_x1[n], in_g[n], ALU.add).then_inc(z_added, 1)

            def variance(t, n):
                dve.wait_ge(z_squared, t + 1)
                dve.tensor_reduce(zvar[n][:], zsq[n], AX_X, ALU.add).then_inc(zvar_ready, 1)
                dve.wait_ge(zstd_ready, t + 1)
                dve.reciprocal(zrstd[n][:], zstd[n][:]).then_inc(zrstd_ready, 1)
                dve.wait_ge(zrstd_ready, t + 1)

            def scale(t, n, first=False):
                if not first:
                    dve.wait_ge(out_done[n], (t // 2) * 16 if isinstance(t, int) else (t - n) * 8)
                dve.tensor_tensor(z_out[n], z[n], rows_b(zrstd[n], TROWS), ALU.mult).then_inc(z_done, 1)

            add(0, 0)
            add(1, 1)
            variance(0, 0)
            scale(0, 0, first=True)
            dve.wait_ge(z_done, 1)
            add(2, 0)
            variance(1, 1)
            scale(1, 1, first=True)
            dve.wait_ge(z_done, 2)
            add(3, 1)
            variance(2, 0)
            scale(2, 0)
            with dve.Fori(2, STEPS // 2) as i:
                for n in range(2):
                    dve.wait_ge(z_done, i * 2 + n - 1)
                    dve.wait_ge(z_in[n], (i + 1) * 32)
                    dve.tensor_tensor(z[n], in_x1[n], in_g[n], ALU.add).then_inc(z_added, 1)
                    variance(i * 2 + n - 1, 1 - n)
                    dve.wait_ge(out_done[1 - n], (i - 1 + n) * 16)
                    dve.tensor_tensor(z_out[1 - n], z[1 - n], rows_b(zrstd[1 - n], TROWS), ALU.mult).then_inc(z_done, 1)
            dve.wait_ge(z_done, STEPS - 2)
            add(STEPS - 1, 0)
            variance(STEPS - 2, 1)
            scale(STEPS - 2, 1)
            variance(STEPS - 1, 0)
            scale(STEPS - 1, 0)


_INS = ["x", "src", "dst", "edge_attr_32", "L0_gnn_u", "L0_gnn_W1", "L0_gnn_b1", "L0_gnn_W2", "L0_gnn_b2", "L1_gnn_W", "L1_gnn_b"]


def kernel(**inputs):
    import numpy as _np
    import concourse.bacc as _bacc
    from concourse import mybir as _mybir
    from concourse.bass_utils import run_bass_kernel_spmd as _run

    nc = _bacc.Bacc("TRN2", target_bir_lowering=False, num_devices=1)
    arrays, args = {}, []
    for name in _INS:
        a = _np.ascontiguousarray(inputs[name])
        arrays[f"in_{name}"] = a
        args.append(nc.dram_tensor(f"in_{name}", a.shape, _mybir.dt.from_np(a.dtype), kind="ExternalInput").ap())
    args.append(nc.dram_tensor("out_0", (NODES, FEAT), F32, kind="ExternalOutput").ap())
    gnn_kernel(nc, *args)
    r = _run(nc, [arrays], core_ids=[0])
    return r.results[0]["out_0"]
```

```python
from contextlib import ExitStack

import numpy as np

import concourse.bass as bass
from concourse import mybir

ALU = mybir.AluOpType
ACT = mybir.ActivationFunctionType
AX_X = mybir.AxisListType.X
F32 = mybir.dt.float32
I32 = mybir.dt.int32

P = 128
NODES, FEAT = 100000, 64
EDGES, EFEAT = 50000, 32
HID = 128
EPS = 1e-5
FLT_MAX = float(np.finfo(np.float32).max)

COLS = 512
LEVELS = 16
ROW_LEVELS = 9
EDGE_PARTS = 100
EDGE_COLS = EDGES // EDGE_PARTS
PAIR_COLS = EDGE_COLS // 2
HALF = NODES // 2
CODE0 = 30 * 256
SIGN_CODE = 65536
PAIR_BITS = 15
PAD = 2.0 ** 120
SKIP = 262144.0

TILES = COLS // P
GROUPS = 98
PER = 2
STEPS = GROUPS // PER
CHUNKS = GROUPS * TILES
STEP_CHUNKS = PER * TILES
PAIR_ROW = 2 * (EFEAT + 2)
DST, SRC = 2 * EFEAT, 2 * EFEAT + 1

TROWS = 16
TILE = P * TROWS
N_PAD = STEPS * TILE
LAST = NODES - (STEPS - 1) * TILE
LAST_PARTS = LAST // TROWS
LN_ROWS = STEP_CHUNKS + TROWS
assert N_PAD >= NODES and LAST_PARTS * TROWS == LAST and GROUPS * COLS >= EDGES

NO_TILE = 64
assert NO_TILE > STEPS
SETTLE = 2
TILE_BITS = TILE.bit_length() - 1
assert TILE == 1 << TILE_BITS

C0_PAIRS = (STEPS - 1) // 2
C0_EARLY = 15
GUARDED = C0_PAIRS - C0_EARLY
assert STEPS % 2 == 1


def gnn_kernel(nc, x, src, dst, edge_attr, u, W1, b1, W2, b2, W, b, out):
    edge_pairs = nc.dram_tensor("edge_pairs", (EDGES // 2, PAIR_ROW), F32, kind="Internal").ap()
    node_rows = nc.dram_tensor("node_rows", (N_PAD, 2, FEAT), F32, kind="Internal").ap()
    x1_table = nc.dram_tensor("x1_table", (N_PAD, FEAT), F32, kind="Internal").ap()
    g_table = nc.dram_tensor("g_table", (N_PAD, FEAT), F32, kind="Internal").ap()
    flags = nc.dram_tensor("flags", (3, P * COLS), F32, kind="Internal").ap()

    node_halves = node_rows.rearrange("n t f -> (n t) f")
    node_pairs = node_rows.rearrange("n t f -> n (t f)")

    with ExitStack() as ctx:
        def sb(name, shape, dt=F32):
            return ctx.enter_context(nc.sbuf_tensor(name, shape, dt))

        def ps(name, shape):
            return ctx.enter_context(nc.psum_tensor(name, shape, F32))

        def sem(name):
            return ctx.enter_context(nc.semaphore(name))

        src_i = sb("src_i", [P, EDGE_COLS], I32)
        dst_i = sb("dst_i", [P, EDGE_COLS], I32)
        src_f = sb("src_f", [P, EDGE_COLS])
        low = sb("low", [P, EDGE_COLS])
        far = sb("far", [P, EDGE_COLS])
        code_i = sb("code_i", [P, EDGE_COLS], I32)
        code_s = sb("code_s", [P, EDGE_COLS], I32)
        pair_i = sb("pair_i", [P, EDGE_COLS], I32)
        pair_tile = sb("pair_tile", [P, PAIR_COLS, PAIR_ROW])
        K = [sb(f"K{n}", [P, COLS]) for n in range(2)]
        KT = [sb(f"KT{n}", [P, COLS]) for n in range(2)]
        part_i = sb("part_i", [P, 1], I32)
        bit_a = sb("bit_a", [P, 8], I32)
        bit_b = sb("bit_b", [P, 8], I32)
        sign = sb("sign", [P, 8])
        flip = sb("flip", [P, 8])
        ident = sb("ident", [P, P])
        row_before = sb("row_before", [1, P + 1])
        row_after = sb("row_after", [1, P])
        edge_words = sb("edge_words", [P, 2])
        edge_codes = sb("edge_codes", [P, 2], I32)
        code_here = sb("code_here", [P, COLS], I32)
        pair_bits = sb("pair_bits", [P, COLS], I32)
        same = sb("same", [P, COLS])
        ends = sb("ends", [P, COLS])
        floor_f = sb("floor_f", [P, COLS])
        pair_f = sb("pair_f", [P, COLS])
        twin = sb("twin", [P, COLS])
        lower = sb("lower", [P, COLS])
        off = sb("off", [P, COLS])
        back2 = sb("back2", [P, COLS])
        node = sb("node", [P, COLS])
        skip = sb("skip", [P, COLS])
        row_f = sb("row_f", [P, COLS])
        one = sb("one", [P, 1])
        count = sb("count", [P, COLS])
        whole = sb("whole", [P, 1])
        row_ends = sb("row_ends", [1, 2 * P])
        row_counts = sb("row_counts", [1, P + 1])
        carry = sb("carry", [P, 1])
        row_node = sb("row_node", [1, P], I32)
        row_tile = sb("row_tile", [1, P], I32)
        settled = sb("settled", [1, STEPS])
        normed = sb("normed", [1, STEPS + 1])
        idle = sb("idle", [1, STEPS])
        plan = sb("plan", [1, STEPS + 1], I32)
        half_tile = sb("half_tile", [1, 1], I32)
        c0_need = sb("c0_need", [1, 1], I32)
        inverse = sb("inverse", [P, COLS])
        pair_idx = sb("pair_idx", [P, GROUPS, TILES], I32)
        row_idx = sb("row_idx", [P, GROUPS, TILES], I32)
        g_idx = sb("g_idx", [P, GROUPS, TILES], I32)
        dst_idx = sb("dst_idx", [P, GROUPS, TILES], I32)
        node_at = sb("node_at", [P, GROUPS, TILES])
        twin_at = sb("twin_at", [P, GROUPS, TILES])
        w1 = sb("w1", [3 * EFEAT, HID])
        w1_u = sb("w1_u", [HID, 1])
        b1_c = sb("b1_c", [HID, 1])
        u0 = sb("u0", [P, 1])
        c1 = sb("c1", [HID, 1])
        c1_relu = sb("c1_relu", [HID, P])
        w2_in = sb("w2_in", [HID, FEAT])
        w2_mean = sb("w2_mean", [HID, 1])
        w2 = sb("w2", [HID, FEAT])
        b2_in = sb("b2_in", [P, FEAT])
        b2_mean = sb("b2_mean", [P, 1])
        b2_b = sb("b2_b", [P, FEAT])
        w_in = sb("w_in", [FEAT, FEAT])
        w_t = sb("w_t", [FEAT, FEAT])
        b_b = sb("b_b", [P, FEAT])
        eps = sb("eps", [P, 1])
        c0_tile = sb("c0_tile", [P, TROWS, FEAT])
        g0_tile = sb("g0_tile", [P, TROWS, FEAT])
        g0_relu = sb("g0_relu", [P, FEAT])
        g0_sum = sb("g0_sum", [P, 1])
        g0_row = sb("g0_row", [P, FEAT])
        idx_in = [sb(f"idx_in{n}", [P, TILES], I32) for n in range(PER)]
        idx_first = [sb(f"idx_first{n}", [P, TILES], I32) for n in range(PER)]
        idx_out = [sb(f"idx_out{n}", [P, TILES], I32) for n in range(PER)]
        pairs = [sb(f"pairs{n}", [P, TILES, PAIR_ROW]) for n in range(PER)]
        wrong = [sb(f"wrong{n}", [P, TILES]) for n in range(PER)]
        odd = [sb(f"odd{n}", [P, TILES], I32) for n in range(PER)]
        same_b = [sb(f"same_b{n}", [FEAT, COLS]) for n in range(PER)]
        floor_b = [sb(f"floor_b{n}", [EFEAT, COLS]) for n in range(PER)]
        feats = [sb(f"feats{n}", [3 * EFEAT, COLS]) for n in range(PER)]
        inverse_b = [sb(f"inverse_b{n}", [EFEAT, COLS]) for n in range(PER)]
        hidden = [sb(f"hidden{n}", [HID, COLS]) for n in range(PER)]
        delta = [sb(f"delta{n}", [P, TILES, FEAT]) for n in range(PER)]
        spare = pair_tile[:].rearrange("p q w -> p (q w)")
        spare_rows = spare[:, 0:PAIR_COLS * PAIR_ROW // FEAT * FEAT].rearrange("p (c f) -> p c f", f=FEAT)
        near = spare_rows[:, 0:2 * LN_ROWS, :].rearrange("p (c t) f -> p c t f", t=2)
        y, ysq, x1 = (spare_rows[:, k * LN_ROWS:(k + 1) * LN_ROWS, :] for k in (2, 3, 4))
        yvar = sb("yvar", [P, LN_ROWS])
        ystd = sb("ystd", [P, LN_ROWS])
        yrstd = sb("yrstd", [P, LN_ROWS])
        aggr = [sb(f"aggr{n}", [FEAT, COLS]) for n in range(PER)]
        gz = sb("gz", [P, STEP_CHUNKS, FEAT])
        gr = sb("gr", [P, STEP_CHUNKS, FEAT])
        gsum = sb("gsum", [P, STEP_CHUNKS])
        gmean = sb("gmean", [P, STEP_CHUNKS])

        def carve(k):
            first = 5 * LN_ROWS + k * TROWS
            return spare_rows[:, first:first + TROWS, :]

        x_tile, xc = carve(0), carve(1)
        xsum = sb("xsum", [P, TROWS])
        xmean = sb("xmean", [P, TROWS])
        in_x1, in_g, z, zsq, z_out = (carve(k) for k in range(5))
        zvar = sb("zvar", [P, TROWS])
        zstd = sb("zstd", [P, TROWS])
        zrstd = sb("zrstd", [P, TROWS])

        p_turn = [ps(f"p_turn{n}", [P, COLS]) for n in range(2)]
        p_feat = [ps(f"p_feat{n}", [FEAT, COLS]) for n in range(PER)]
        p_hid = [ps(f"p_hid{n}", [HID, COLS]) for n in range(PER)]
        p_rows_banks = ps("p_rows", [P, PER * COLS])
        p_rows = p_rows_banks[:].rearrange("p (n t f) -> p n t f", n=PER, f=FEAT)[:, :, 0:TILES, :]

        pool_stands, pe_stands, dve_stands = sem("pool_stands"), sem("pe_stands"), sem("dve_stands")
        sp_stands = sem("sp_stands")
        src_in, dst_in, attr_in = sem("src_in"), sem("dst_in"), sem("attr_in")
        weights_in = sem("weights_in")
        ident_zero, ident_done = sem("ident_zero"), sem("ident_done")
        pair_iota, part_iota = sem("pair_iota"), sem("part_iota")
        setup = sem("setup")
        w_turned, w_t_ready = sem("w_turned"), sem("w_t_ready")
        c1_ready, c1_relu_ready = sem("c1_ready"), sem("c1_relu_ready")
        c0_psum, c0_ready, g0_ready = sem("c0_psum"), sem("c0_ready"), sem("g0_ready")
        g0_relu_done = sem("g0_relu_done")
        pair_ids, pairs_out = sem("pair_ids"), sem("pairs_out")
        sorting = sem("sorting")
        turn_ready, sort_done = sem("turn_ready"), sem("sort_done")
        turned, untangled = sem("turned"), sem("untangled")
        edges_turned, edges_shifted, edges_back = sem("edges_turned"), sem("edges_shifted"), sem("edges_back")
        flags_ready, flags_out, inverse_out = sem("flags_ready"), sem("flags_out"), sem("inverse_out")
        idx_turned, idx_kept = sem("idx_turned"), sem("idx_kept")
        pairs_known = sem("pairs_known")
        counts_local, counts_turned, rows_counted, carry_turned, inverse_ready = (
            sem("counts_local"), sem("counts_turned"), sem("rows_counted"), sem("carry_turned"), sem("inverse_ready"))
        plan_ready, c0_need_ready = sem("plan_ready"), sem("c0_need_ready")
        tables = sem("tables")
        c0_out, c0_last_out = [sem(f"c0_out{n}") for n in range(2)], sem("c0_last_out")
        g0_out, x_in, x_out = sem("g0_out"), sem("x_in"), sem("x_out")
        xsum_ready, xmean_ready, xc_ready = sem("xsum_ready"), sem("xmean_ready"), sem("xc_ready")
        first_idx = [sem(f"first_idx{n}") for n in range(PER)]
        in_idx = [sem(f"in_idx{n}") for n in range(PER)]
        out_idx = [sem(f"out_idx{n}") for n in range(PER)]
        gathered = [sem(f"gathered{n}") for n in range(PER)]
        scattered = [sem(f"scattered{n}") for n in range(PER)]
        flags_in = [sem(f"flags_in{n}") for n in range(PER)]
        inverse_in = [sem(f"inverse_in{n}") for n in range(PER)]
        edge_known, edge_odd, edge_picked = sem("edge_known"), sem("edge_odd"), sem("edge_picked")
        dst_picked, dst_kept = sem("dst_picked"), sem("dst_kept")
        attrs_turned = sem("attrs_turned")
        summed, maxed, averaged = sem("summed"), sem("maxed"), sem("averaged")
        hid_psum, hid_ready, delta_psum, delta_ready = sem("hid_psum"), sem("hid_ready"), sem("delta_psum"), sem("delta_ready")
        g_idx_ready = sem("g_idx_ready")
        l1_in_idx = [sem(f"l1_in_idx{n}") for n in range(PER)]
        l1_out_idx = [sem(f"l1_out_idx{n}") for n in range(PER)]
        l1_gathered, l1_scattered = sem("l1_gathered"), sem("l1_scattered")
        l1_flags_in = [sem(f"l1_flags_in{n}") for n in range(PER)]
        tile_in = sem("tile_in")
        y_ready = sem("y_ready")
        ysq_ready, yvar_ready, ystd_ready, yrstd_ready = sem("ysq_ready"), sem("yvar_ready"), sem("ystd_ready"), sem("yrstd_ready")
        x1_ready, x1_out = sem("x1_ready"), sem("x1_out")
        x1_turned, aggr_ready, g_psum = sem("x1_turned"), sem("aggr_ready"), sem("g_psum")
        gz_ready, gr_ready, gsum_ready, gmean_ready, g_ready = sem("gz_ready"), sem("gr_ready"), sem("gsum_ready"), sem("gmean_ready"), sem("g_ready")
        z_in = sem("z_in")
        z_added, z_squared, zvar_ready, zstd_ready, zrstd_ready, z_done = (
            sem("z_added"), sem("z_squared"), sem("zvar_ready"), sem("zstd_ready"), sem("zrstd_ready"), sem("z_done"))
        out_done = sem("out_done")

        block = ctx.enter_context(nc.Block())

        def group_of(s, n):
            g = s * PER + n
            return bass.ds(g, 1) if not isinstance(g, int) else slice(g, g + 1)

        def tile_rows(t, parts=P):
            r = t * TILE
            return slice(r, r + parts * TROWS) if isinstance(t, int) else bass.ds(r, parts * TROWS)

        def planned(tile):
            return nc.s_assert_within(tile, 0, STEPS - SETTLE - 2, skip_runtime_bounds_check_because=
                                      "plan holds NO_TILE or more where the branch is not taken, else a tile before the last")

        @block.sync
        def _(sp):
            sp.dma_start(src_i[0:EDGE_PARTS, :], src.rearrange("(p c) -> p c", p=EDGE_PARTS)).then_inc(src_in, 16)
            sp.dma_start(w1_u[:], W1[3 * EFEAT, :].rearrange("(h a) -> h a", a=1)).then_inc(weights_in, 16)
            sp.dma_start(b1_c[:], b1.rearrange("(h a) -> h a", a=1)).then_inc(weights_in, 16)
            sp.dma_start(u0[:], u[0, :].partition_broadcast(P)).then_inc(weights_in, 16)
            sp.dma_start(w2_in[:], W2).then_inc(weights_in, 16)
            sp.dma_start(b2_in[:], b2.partition_broadcast(P)).then_inc(weights_in, 16)
            sp.dma_start(b_b[:], b.partition_broadcast(P)).then_inc(weights_in, 16)
            sp.dma_start(w1[:], W1[0:3 * EFEAT, :]).then_inc(weights_in, 16)
            sp.dma_start(w_in[:], W).then_inc(weights_in, 16)
            sp.dma_start(dst_i[0:EDGE_PARTS, :], dst.rearrange("(p c) -> p c", p=EDGE_PARTS)).then_inc(dst_in, 16)
            sp.dma_start(pair_tile[0:EDGE_PARTS, :, 0:2 * EFEAT],
                         edge_attr.rearrange("(p q t) f -> p q (t f)", p=EDGE_PARTS, t=2)).then_inc(attr_in, 16)
            sp.wait_ge(attr_in, 16)
            sp.wait_ge(pair_ids, 2)
            sp.dma_start(edge_pairs.rearrange("(p q) w -> p q w", p=EDGE_PARTS),
                         pair_tile[0:EDGE_PARTS]).then_inc(pairs_out, 16)

            def first_delta(t, out):
                sp.dma_start(node_rows[tile_rows(t), 1, :].rearrange("(p c) f -> p c f", p=P),
                             c0_tile[:]).then_inc(out, 16)

            def first_pair(i):
                for n in range(2):
                    sp.wait_ge(c0_out[n], i * 16)
                    first_delta(i * 2 + n, c0_out[n])

            sp.wait_ge(c0_ready, 1)
            first_delta(STEPS - 1, c0_last_out)
            first_delta(0, c0_out[0])
            first_delta(1, c0_out[1])
            with sp.Fori(1, C0_EARLY) as i:
                first_pair(i)

            def load_flags(target, row, s, n, ready):
                at = (s * PER + n) * COLS
                cols = slice(at, at + COLS) if isinstance(at, int) else bass.ds(at, COLS)
                sp.dma_start(target, flags[row, cols].partition_broadcast(target.shape[0])).then_inc(ready[n], 16)

            def load_idx(slot, table, s, n, ready):
                sp.dma_start(slot[n][:], table[:, group_of(s, n), :].rearrange("p a t -> p (a t)")).then_inc(ready[n], 16)

            def l0_idx_in(s):
                for n in range(PER):
                    sp.wait_ge(gathered[n], s * 16 * TILES)
                    load_idx(idx_in, pair_idx, s, n, in_idx)

            def l0_idx_out(s, first=False):
                for n in range(PER):
                    if first:
                        sp.wait_ge(idx_kept, 4)
                    else:
                        sp.wait_ge(scattered[n], s * 16 * TILES)
                    load_idx(idx_out, row_idx, s, n, out_idx)

            def l0_flags(s, first=False):
                for n in range(PER):
                    if first:
                        sp.wait_ge(flags_out, 32)
                    else:
                        sp.wait_ge(summed, (s - 1) * PER + n + 1)
                        sp.wait_ge(maxed, (s - 1) * PER + n + 1)
                    load_flags(same_b[n][0:EFEAT, :], 0, s, n, flags_in)
                    load_flags(floor_b[n][:], 1, s, n, flags_in)
                for n in range(PER):
                    if first:
                        sp.wait_ge(inverse_out, 16)
                    else:
                        sp.wait_ge(averaged, (s - 1) * PER + n + 1)
                    load_flags(inverse_b[n][:], 2, s, n, inverse_in)

            def l0_x(s, first=False, parts=P):
                if not first:
                    sp.wait_ge(xc_ready, s)
                sp.dma_start(x_tile[0:parts], x[tile_rows(s, parts), :].rearrange("(p c) f -> p c f", p=parts)).then_inc(x_in, 16)

            def l0_sp(s, parts=P):
                l0_idx_in(s)
                l0_idx_out(s - 1)
                l0_flags(s)
                l0_x(s, parts=parts)

            sp.wait_ge(idx_kept, 1)
            for n in range(PER):
                load_idx(idx_first, pair_idx, 0, n, first_idx)
            for n in range(PER):
                load_idx(idx_in, pair_idx, 1, n, in_idx)
            sp.wait_ge(pairs_out, 16)
            l0_x(0, first=True)
            first_pair(C0_EARLY)
            sp.wait_ge(c0_need_ready, 1)
            need = sp.value_load(c0_need[:], min_val=1, max_val=C0_PAIRS)
            with sp.If(need > C0_EARLY):
                with sp.Fori(C0_EARLY + 1, C0_PAIRS) as i:
                    first_pair(i)
            with sp.Else():
                sp.sem_inc(sp_stands, 1)

            def late_pair(i):
                with sp.If(need > C0_EARLY):
                    sp.sem_inc(sp_stands, 1)
                with sp.Else():
                    first_pair(i)

            l0_flags(0, first=True)
            l0_idx_out(0, first=True)
            l0_flags(1)
            l0_idx_in(2)
            late_pair(C0_EARLY + 1)
            l0_x(1)
            l0_flags(2)
            late_pair(C0_EARLY + 2)
            l0_idx_out(1)
            l0_x(2)
            with sp.Fori(3, GUARDED) as s:
                late_pair(s + C0_EARLY)
                l0_sp(s)
            with sp.Fori(GUARDED, STEPS - 1) as s:
                l0_sp(s)
            l0_sp(STEPS - 1, LAST_PARTS)
            l0_idx_out(STEPS - 1)

            def l1_idx(s):
                for n in range(PER):
                    load_idx(idx_in, dst_idx, s, n, l1_in_idx)

            def l1_load(s):
                if not (isinstance(s, int) and s == 0):
                    sp.wait_ge(l1_gathered, s * 16 * STEP_CHUNKS)
                    l1_idx(s)
                if not (isinstance(s, int) and s == 0):
                    sp.wait_ge(y_ready, s)
                sp.dma_start(near[:, STEP_CHUNKS:, :, :],
                             node_rows[tile_rows(s)].rearrange("(p c) t f -> p c t f", p=P)).then_inc(tile_in, 16)

            def l1_keep(s):
                sp.wait_ge(x1_ready, (s + 1) * 2)
                sp.dma_start(x1_table[tile_rows(s), :].rearrange("(p c) f -> p c f", p=P),
                             x1[:, STEP_CHUNKS:, :]).then_inc(x1_out, 16)

            def l1_flags(s):
                for n in range(PER):
                    if not (isinstance(s, int) and s == 0):
                        sp.wait_ge(aggr_ready, (s - 1) * PER + n + 1)
                    load_flags(same_b[n][:], 0, s, n, l1_flags_in)

            def l1_out(s):
                if not (isinstance(s, int) and s == 0):
                    sp.wait_ge(l1_scattered, s * 16 * STEP_CHUNKS)
                for n in range(PER):
                    load_idx(idx_out, g_idx, s, n, l1_out_idx)

            def norm_load_x1(t):
                sp.wait_ge(z_added, t + 1)
                sp.sem_inc(sp_stands, 1)
                sp.wait_ge(x1_out, (t + 1) * 16)
                sp.sem_inc(sp_stands, 1)
                sp.dma_start(in_x1, x1_table[tile_rows(t), :].rearrange("(p c) f -> p c f", p=P)).then_inc(z_in, 16)

            def norm_load_g(t):
                sp.dma_start(in_g, g_table[tile_rows(t), :].rearrange("(p c) f -> p c f", p=P)).then_inc(z_in, 16)

            def norm_load(t):
                norm_load_x1(t)
                norm_load_g(t)

            sp.wait_ge(plan_ready, 1)
            sp.wait_ge(dst_kept, GROUPS)
            l1_idx(0)
            sp.wait_ge(averaged, GROUPS)
            l1_flags(0)
            sp.wait_ge(g_idx_ready, 1)
            sp.wait_ge(x_out, 16 * STEPS)
            for n in range(PER):
                sp.wait_ge(scattered[n], 16 * TILES * STEPS)
            l1_load(0)
            l1_out(0)
            l1_load(1)
            l1_keep(0)
            l1_flags(1)
            l1_load(2)
            l1_keep(1)
            l1_flags(2)
            def l1_sp(s, tile=None):
                l1_load(s + 1)
                l1_out(s - 1)
                if tile is not None:
                    norm_load(tile)
                l1_keep(s)
                l1_flags(s + 1)

            with sp.Fori(2, STEPS - 1) as s:
                tile = sp.value_load(plan[0:1, bass.ds(s + 1, 1)], min_val=0, max_val=NO_TILE + STEPS)
                with sp.If(tile < NO_TILE):
                    l1_sp(s, planned(tile))
                with sp.Else():
                    l1_sp(s)
            l1_keep(STEPS - 1)
            l1_out(STEPS - 2)
            l1_out(STEPS - 1)

            done = sp.value_load(plan[0:1, STEPS:STEPS + 1], min_val=0, max_val=STEPS - SETTLE - 1)
            norm_load_x1(done)
            sp.wait_ge(l1_scattered, 16 * STEP_CHUNKS * STEPS)
            with sp.Fori(done, STEPS - 2) as t:
                norm_load_g(t)
                norm_load_x1(t + 1)
            norm_load_g(STEPS - 2)
            norm_load(STEPS - 1)

        @block.gpsimd
        def _(pool):
            pool.iota(pair_i[:], pattern=[[1, PAIR_COLS], [0, 2]], base=0,
                      channel_multiplier=PAIR_COLS).then_inc(pair_iota, 1)
            pool.iota(part_i[:], pattern=[[0, 1]], base=0, channel_multiplier=1).then_inc(part_iota, 1)
            pool.memset(ident[:], 0.0).then_inc(ident_zero, 1)
            pool.wait_ge(ident_zero, 1)
            pool.affine_select(out=ident[:], in_=ident[:], compare_op=ALU.not_equal, fill=1.0, base=0,
                               pattern=[[-1, P]], channel_multiplier=1).then_inc(ident_done, 1)

            def gather(n, target, table, top, ready, slot=idx_in):
                pool.sem_inc(pool_stands, 1)
                for t in range(TILES):
                    pool.indirect_dma_start(out=target(t), out_offset=None, in_=table,
                                            in_offset=bass.IndirectOffsetOnAxis(ap=slot[n][:, t:t + 1], axis=0),
                                            bounds_check=top, oob_is_err=False).then_inc(ready, 16)

            def scatter(n, source, table, top, ready):
                pool.sem_inc(pool_stands, 1)
                for t in range(TILES):
                    pool.indirect_dma_start(out=table, in_=source(t), in_offset=None,
                                            out_offset=bass.IndirectOffsetOnAxis(ap=idx_out[n][:, t:t + 1], axis=0),
                                            bounds_check=top, oob_is_err=False).then_inc(ready, 16)

            def l0_gather(s, first=False):
                for n in range(PER):
                    if first:
                        pool.wait_ge(first_idx[n], 16)
                    else:
                        pool.wait_ge(in_idx[n], s * 16)
                        pool.wait_ge(attrs_turned, (s - 1) * PER + n + 1)
                        pool.wait_ge(dst_kept, (s - 1) * PER + n + 1)
                    gather(n, lambda t, n=n: pairs[n][:, t, :], edge_pairs, EDGES // 2 - 1, gathered[n],
                           idx_first if first else idx_in)

            def l0_scatter(s):
                for n in range(PER):
                    pool.wait_ge(out_idx[n], (s + 1) * 16)
                    pool.wait_ge(delta_ready, s * PER + n + 1)
                    scatter(n, lambda t, n=n: delta[n][:, t, :], node_halves, 2 * N_PAD - 1, scattered[n])

            pool.wait_ge(pairs_out, 16)
            l0_gather(0, first=True)
            l0_gather(1)
            l0_gather(2)
            pool.wait_ge(c0_need_ready, 1)
            need = pool.value_load(c0_need[:], min_val=1, max_val=C0_PAIRS)
            pool.wait_ge(c0_last_out, 16)
            pool.sem_inc(pool_stands, 1)
            for n in range(2):
                pool.wait_ge(c0_out[n], need * 16)
                pool.sem_inc(pool_stands, 1)
            l0_scatter(0)
            l0_scatter(1)
            with pool.Fori(3, GUARDED + 1) as s:
                l0_gather(s)
                l0_scatter(s - 1)
            for n in range(2):
                pool.wait_ge(c0_out[n], 16 * C0_PAIRS)
            with pool.Fori(GUARDED + 1, STEPS) as s:
                l0_gather(s)
                l0_scatter(s - 1)
            l0_scatter(STEPS - 1)

            for n in range(PER):
                pool.wait_ge(scattered[n], 16 * TILES * STEPS)
            pool.wait_ge(x_out, 16 * STEPS)

            def l1_gather(s, first=False):
                if not first:
                    pool.wait_ge(y_ready, s)
                for n in range(PER):
                    pool.wait_ge(l1_in_idx[n], (s + 1) * 16)
                    gather(n, lambda t, n=n: near[:, n * TILES + t, :, :].rearrange("p t f -> p (t f)"),
                           node_pairs, N_PAD - 1, l1_gathered)

            def l1_scatter(s):
                pool.wait_ge(g_ready, s + 1)
                for n in range(PER):
                    pool.wait_ge(l1_out_idx[n], (s + 1) * 16)
                    scatter(n, lambda t, n=n: delta[n][:, t, :], g_table, N_PAD - 1, l1_scattered)

            l1_gather(0, first=True)
            l1_gather(1)
            pool.wait_ge(g0_out, 16 * STEPS)
            with pool.Fori(2, STEPS) as s:
                l1_gather(s)
                l1_scatter(s - 2)
            l1_scatter(STEPS - 2)
            l1_scatter(STEPS - 1)

        @block.scalar
        def _(act):
            act.wait_ge(weights_in, 16 * 8)
            act.activation(g0_relu[:], b_b[:], ACT.Relu).then_inc(g0_relu_done, 1)

            act.wait_ge(attr_in, 16)
            act.wait_ge(dst_in, 16)
            ids = pair_tile[0:EDGE_PARTS, :, DST:PAIR_ROW].rearrange("p q (t w) -> p q t w", t=2)
            act.activation(ids[:, :, :, 0],
                           dst_i[0:EDGE_PARTS, :].rearrange("p (q t) -> p q t", t=2), ACT.Copy).then_inc(pair_ids, 1)
            act.wait_ge(src_in, 16)
            act.activation(ids[:, :, :, 1],
                           src_i[0:EDGE_PARTS, :].rearrange("p (q t) -> p q t", t=2), ACT.Copy).then_inc(pair_ids, 1)

            for n in range(2 * (LEVELS - ROW_LEVELS)):
                act.wait_ge(turned, n + 1)
                to = KT[0] if n % 2 == 0 else K[0]
                act.activation(to[:], p_turn[n % 2][:], ACT.Copy).then_inc(untangled, 1)


            def keep_table(n, to):
                act.wait_ge(idx_turned, n + 1)
                turned_v = p_turn[n % 2][:].rearrange("p (t g) -> p g t", t=TILES)
                act.activation(to[:], turned_v[:, 0:GROUPS, :], ACT.Copy).then_inc(idx_kept, 1)

            keep_table(0, pair_idx)
            act.wait_ge(flags_ready, 1)
            act.dma_start(flags[0, :].rearrange("(p c) -> p c", p=P), same[:]).then_inc(flags_out, 16)
            act.dma_start(flags[1, :].rearrange("(p c) -> p c", p=P), floor_f[:]).then_inc(flags_out, 16)
            for n, to in enumerate((node_at, twin_at, row_idx)):
                keep_table(n + 1, to)
            act.wait_ge(inverse_ready, 1)
            act.dma_start(flags[2, :].rearrange("(p c) -> p c", p=P), inverse[:]).then_inc(inverse_out, 16)

            def l0_hidden(s, first=False):
                for n in range(PER):
                    act.wait_ge(hid_psum, s * PER + n + 1)
                    if not first:
                        act.wait_ge(delta_psum, (s - 1) * PER + n + 1)
                    act.activation(hidden[n][:], p_hid[n][:], ACT.Relu, bias=c1[:, 0:1]).then_inc(hid_ready, 1)
                act.dma_start(g_table[tile_rows(s), :].rearrange("(p c) f -> p c f", p=P), g0_tile[:]).then_inc(g0_out, 16)
                act.wait_ge(xc_ready, s + 1)
                act.dma_start(node_rows[tile_rows(s), 0, :].rearrange("(p c) f -> p c f", p=P), xc).then_inc(x_out, 16)

            act.wait_ge(setup, 1)
            act.wait_ge(g0_ready, 1)
            act.wait_ge(c1_ready, 1)
            l0_hidden(0, first=True)
            with act.Fori(1, STEPS) as s:
                l0_hidden(s)

            def l1_square(s):
                act.wait_ge(y_ready, s + 1)
                act.activation(ysq, y, ACT.Square).then_inc(ysq_ready, 1)

            def l1_relu(s):
                act.wait_ge(gz_ready, s + 1)
                act.activation(gr[:], gz[:], ACT.Relu).then_inc(gr_ready, 1)

            def l1_deviation(s):
                act.wait_ge(yvar_ready, s + 1)
                act.activation(ystd[:], yvar[:], ACT.Sqrt, bias=eps[:, 0:1], scale=1.0 / FEAT).then_inc(ystd_ready, 1)

            def norm_square(t):
                act.wait_ge(z_added, t + 2)
                act.activation(zsq, z, ACT.Square).then_inc(z_squared, 1)

            def norm_deviation(t):
                act.wait_ge(zvar_ready, t + 1)
                act.activation(zstd[:], zvar[:], ACT.Sqrt, bias=eps[:, 0:1], scale=1.0 / FEAT).then_inc(zstd_ready, 1)

            def norm_store(t, parts=P):
                act.wait_ge(z_done, t + 2)
                act.dma_start(out[tile_rows(t, parts), :].rearrange("(p c) f -> p c f", p=parts),
                              z_out[0:parts]).then_inc(out_done, 16)

            def l1_act(s, tile=None):
                l1_square(s)
                if tile is not None:
                    norm_square(tile)
                l1_relu(s - 1)
                l1_deviation(s)
                if tile is not None:
                    norm_deviation(tile)
                    norm_store(tile)

            act.sem_inc(out_done, 16)
            l1_square(0)
            l1_deviation(0)
            l1_act(1)
            act.wait_ge(plan_ready, 1)
            with act.Fori(2, STEPS) as s:
                tile = act.value_load(plan[0:1, bass.ds(s, 1)], min_val=0, max_val=NO_TILE + STEPS)
                with act.If(tile < NO_TILE):
                    l1_act(s, planned(tile))
                with act.Else():
                    l1_act(s)
            l1_relu(STEPS - 1)

            done = act.value_load(plan[0:1, STEPS:STEPS + 1], min_val=0, max_val=STEPS - SETTLE - 1)
            with act.Fori(done, STEPS - 1) as t:
                norm_square(t)
                norm_deviation(t)
                norm_store(t)
            norm_square(STEPS - 1)
            norm_deviation(STEPS - 1)
            norm_store(STEPS - 1, LAST_PARTS)
            act.wait_ge(out_done, 16 * (STEPS + 1))

        @block.tensor
        def _(pe):
            pe.wait_ge(ident_done, 1)
            pe.wait_ge(weights_in, 16 * 8)
            pe.transpose(p_hid[0][0:FEAT, 0:FEAT], w_in[:], ident[0:FEAT, 0:FEAT]).then_inc(w_turned, 1)
            for n in range(2 * (LEVELS - ROW_LEVELS)):
                pe.wait_ge(turn_ready, n + 1)
                if n % 2:
                    from_ = KT[(n // 2 + 1) % 2]
                else:
                    from_ = K[1 if n == 0 else 0]
                for t in range(TILES):
                    ins = pe.transpose(p_turn[n % 2][:, t * P:(t + 1) * P], from_[:, t * P:(t + 1) * P], ident[:])
                ins.then_inc(turned, 1)
                if n == 0:
                    pe.wait_ge(c1_relu_ready, 1)
                    pe.matmul(p_rows[:, 0, 0, :], c1_relu[:], w2[:], start=True, stop=True).then_inc(c0_psum, 1)
            def turn_table(n, from_):
                for t in range(TILES):
                    ins = pe.transpose(p_turn[n % 2][:, t * P:(t + 1) * P], from_[:, t * P:(t + 1) * P], ident[:])
                ins.then_inc(idx_turned, 1)

            pe.wait_ge(sort_done, 1)
            pe.transpose(p_hid[0][0:1, 0:P], K[1][:, COLS - 1:COLS], ident[:])
            pe.transpose(p_hid[0][0:1, P:2 * P], K[1][:, 0:1], ident[:]).then_inc(edges_turned, 1)
            pe.wait_ge(pairs_known, 1)
            turn_table(0, pair_f)
            pe.wait_ge(edges_shifted, 1)
            pe.transpose(p_hid[0][:, 2 * P:2 * P + 1], row_before[0:1, 0:P], ident[0:1, 0:1])
            pe.transpose(p_hid[0][:, 2 * P + 1:2 * P + 2], row_after[0:1, 0:P], ident[0:1, 0:1]).then_inc(edges_back, 1)

            pe.wait_ge(counts_local, 1)
            pe.transpose(p_hid[1][0:1, 0:P], count[:, COLS - 1:COLS], ident[:])
            pe.transpose(p_hid[1][0:1, P:2 * P], whole[:], ident[:])
            pe.transpose(p_hid[1][0:1, 2 * P:3 * P], node[:, 0:1], ident[:]).then_inc(counts_turned, 1)
            pe.wait_ge(rows_counted, 1)
            pe.transpose(p_hid[1][:, 3 * P:3 * P + 1], row_counts[0:1, 0:P], ident[0:1, 0:1]).then_inc(carry_turned, 1)

            pe.wait_ge(tables, 1)
            for n, from_ in enumerate((node, twin, row_f)):
                if n >= 1:
                    pe.wait_ge(idx_kept, n)
                turn_table(n + 1, from_)

            def l0_turn(s, n, first=False):
                pe.wait_ge(edge_picked, s * PER + n + 1)
                if not first:
                    pe.wait_ge(maxed, (s - 1) * PER + n + 1)
                for t in range(TILES):
                    ins = pe.transpose(p_feat[n][0:EFEAT, t * P:(t + 1) * P], pairs[n][:, t, 0:EFEAT], ident[:])
                ins.then_inc(attrs_turned, 1)

            def l0_mlp_in(s, n, first=False):
                pe.wait_ge(averaged, s * PER + n + 1)
                if not first:
                    pe.wait_ge(hid_ready, (s - 1) * PER + n + 1)
                pe.matmul(p_hid[n][:], w1[:], feats[n][:], start=True, stop=True).then_inc(hid_psum, 1)

            def l0_mlp_out(s, n, first=False):
                pe.wait_ge(hid_ready, s * PER + n + 1)
                if not first:
                    pe.wait_ge(delta_ready, (s - 1) * PER + n + 1)
                for t in range(TILES):
                    ins = pe.matmul(p_rows[:, n, t, :], hidden[n][:, t * P:(t + 1) * P], w2[:],
                                    start=True, stop=True)
                ins.then_inc(delta_psum, 1)

            def l0_pe(s, first=False):
                l0_turn(s, 0, first)
                l0_mlp_in(s, 0, first)
                l0_turn(s, 1, first)
                l0_mlp_out(s, 0, first)
                l0_mlp_in(s, 1, first)
                l0_mlp_out(s, 1, first)

            pe.wait_ge(weights_in, 16 * 8)
            pe.wait_ge(c0_ready, 1)
            pe.wait_ge(w_t_ready, 1)
            l0_pe(0, first=True)
            with pe.Fori(1, STEPS) as s:
                l0_pe(s)

            def l1_pe(s, first=False):
                pe.wait_ge(x1_ready, s * 2 + 1)
                for n in range(PER):
                    if not first:
                        pe.wait_ge(aggr_ready, (s - 1) * PER + n + 1)
                    pe.sem_inc(pe_stands, 1)
                    for t in range(TILES):
                        ins = pe.transpose(p_feat[n][:, t * P:(t + 1) * P], x1[:, n * TILES + t, :], ident[:])
                    ins.then_inc(x1_turned, 1)
                for n in range(PER):
                    pe.wait_ge(aggr_ready, s * PER + n + 1)
                    if not first and n == 0:
                        pe.wait_ge(gz_ready, s)
                    for t in range(TILES):
                        ins = pe.matmul(p_rows[:, n, t, :], aggr[n][:, t * P:(t + 1) * P], w_t[:],
                                        start=True, stop=True)
                    ins.then_inc(g_psum, 1)

            pe.wait_ge(delta_ready, GROUPS)
            l1_pe(0, first=True)
            with pe.Fori(1, STEPS) as s:
                l1_pe(s)

        @block.vector
        def _(dve):
            steps = [0]

            def link(ins):
                steps[0] += 1
                ins.then_inc(sorting, 1)
                dve.wait_ge(sorting, steps[0])

            def mark(ins):
                steps[0] += 1
                ins.then_inc(sorting, 1)

            mark(dve.memset(one[:], 1.0))
            mark(dve.memset(row_counts[:, 0:1], 0.0))
            mark(dve.memset(feats[1][:, COLS - 1:COLS], 0.0))
            mark(dve.memset(aggr[1][:, COLS - 1:COLS], 0.0))
            dve.memset(eps[:], EPS).then_inc(setup, 1)
            mark(dve.memset(row_before[:], PAD))
            mark(dve.memset(row_after[:], PAD))
            link(dve.memset(K[0][:], PAD))
            q = slice(0, EDGE_PARTS)
            dve.wait_ge(src_in, 16)
            link(dve.tensor_copy(src_f[q, :], src_i[q, :]))
            mark(dve.tensor_scalar(low[q, :], src_f[q, :], float(HALF), float(SIGN_CODE), ALU.is_lt, ALU.mult))
            link(dve.tensor_scalar(far[q, :], src_f[q, :], HALF - 0.5, None, ALU.subtract))
            link(dve.scalar_tensor_tensor(out=far[q, :], in0=far[q, :], scalar=-1.0, in1=far[q, :],
                                          op0=ALU.mult, op1=ALU.max))
            link(dve.scalar_tensor_tensor(out=code_i[q, :], in0=far[q, :], scalar=CODE0 - 0.5, in1=low[q, :],
                                          op0=ALU.add, op1=ALU.add))
            link(dve.tensor_scalar(code_s[q, :], code_i[q, :], PAIR_BITS, None, ALU.logical_shift_left))
            dve.wait_ge(pair_iota, 1)
            link(dve.tensor_tensor(K[0][q, 0:EDGE_COLS].bitcast(I32), code_s[q, :], pair_i[q, :], ALU.bitwise_or))
            dve.wait_ge(part_iota, 1)
            for bit in range(8):
                mark(dve.tensor_scalar(bit_a[:, bit:bit + 1], part_i[:], bit, None, ALU.logical_shift_right))
            dve.wait_ge(sorting, steps[0])
            link(dve.tensor_scalar(bit_b[:], bit_a[:], 1, None, ALU.bitwise_and))
            link(dve.tensor_scalar(sign[:], bit_b[:], -2.0, 1.0, ALU.mult, ALU.add))
            link(dve.tensor_tensor(flip[:, 0:7], sign[:, 0:7], sign[:, 1:8], ALU.mult))
            link(dve.tensor_scalar(K[1][:], K[0][:], sign[:, 0:1], None, ALU.mult))

            def exchange(bufs, cur, dist, mirrored=False, ends_phase=None):
                a = bufs[cur][:].rearrange("p (a t d) -> p a t d", t=2, d=dist)
                o = bufs[1 - cur][:].rearrange("p (a t d) -> p a t d", t=2, d=dist)
                left, right = a[:, :, 0, :], a[:, :, 1, :]
                back = slice(None, None, -1) if mirrored and dist > 1 else slice(None)
                dve.tensor_tensor(o[:, :, 0, :], left, right[:, :, back], ALU.min)
                ins = dve.tensor_tensor(o[:, :, 1, :], right, left[:, :, back], ALU.max)
                if ends_phase is not None:
                    ins.then_inc(ends_phase, 1)
                else:
                    link(ins)
                return 1 - cur

            def constants():
                dve.wait_ge(weights_in, 16 * 8)
                mark(dve.tensor_reduce(w2_mean[:], w2_in[:], AX_X, ALU.add))
                link(dve.tensor_reduce(b2_mean[:], b2_in[:], AX_X, ALU.add))
                mark(dve.tensor_scalar(w2_mean[:], w2_mean[:], 1.0 / FEAT, None, ALU.mult))
                link(dve.tensor_scalar(b2_mean[:], b2_mean[:], 1.0 / FEAT, None, ALU.mult))
                mark(dve.tensor_scalar(w2[:], w2_in[:], w2_mean[:, 0:1], None, ALU.subtract))
                link(dve.tensor_scalar(b2_b[:], b2_in[:], b2_mean[:, 0:1], None, ALU.subtract))
                dve.tensor_scalar(c1[:], w1_u[:], u0[:, 0:1], b1_c[:, 0:1], ALU.mult, ALU.add).then_inc(c1_ready, 1)
                dve.wait_ge(c1_ready, 1)
                dve.tensor_scalar(c1_relu[:], c1[:, 0:1].broadcast_to([HID, P]), 0.0, None, ALU.max).then_inc(c1_relu_ready, 1)
                dve.wait_ge(g0_relu_done, 1)
                link(dve.tensor_reduce(g0_sum[:], g0_relu[:], AX_X, ALU.add))
                link(dve.tensor_scalar(g0_sum[:], g0_sum[:], 1.0 / FEAT, None, ALU.mult))
                link(dve.tensor_scalar(g0_row[:], g0_relu[:], g0_sum[:, 0:1], None, ALU.subtract))
                dve.tensor_copy(g0_tile[:], g0_row[:].unsqueeze(1).broadcast_to([P, TROWS, FEAT])).then_inc(g0_ready, 1)
                dve.wait_ge(c0_psum, 1)
                dve.tensor_tensor(c0_tile[:], p_rows[:, 0, 0:1, :].broadcast_to([P, TROWS, FEAT]),
                                  b2_b[:].unsqueeze(1).broadcast_to([P, TROWS, FEAT]), ALU.add).then_inc(c0_ready, 1)
                dve.wait_ge(w_turned, 1)
                dve.tensor_copy(w_t[:], p_hid[0][0:FEAT, 0:FEAT]).then_inc(w_t_ready, 1)

            cur = 1
            for level in range(1, ROW_LEVELS + 1):
                cur = exchange(K, cur, 2 ** (level - 1), mirrored=True)
                for d in range(level - 2, -1, -1):
                    cur = exchange(K, cur, 2 ** d)
            for level in range(ROW_LEVELS + 1, LEVELS + 1):
                m = level - ROW_LEVELS - 1
                dve.tensor_scalar(K[1 - cur][:], K[cur][:], flip[:, m:m + 1], None, ALU.mult).then_inc(turn_ready, 1)
                if m == 0:
                    constants()
                dve.wait_ge(untangled, 2 * m + 1)
                cur = 0
                for d in range(m, -1, -1):
                    cur = exchange(KT, cur, 2 ** d, ends_phase=turn_ready if d == 0 else None)
                dve.wait_ge(untangled, 2 * m + 2)
                cur = 0
                for d in range(ROW_LEVELS - 1, -1, -1):
                    cur = exchange(K, cur, 2 ** d, ends_phase=sort_done if d == 0 and level == LEVELS else None)
            dve.wait_ge(sort_done, 1)

            here = K[1]
            mark(dve.tensor_scalar(code_here[:], here[:].bitcast(I32), PAIR_BITS, None, ALU.logical_shift_right))
            link(dve.tensor_scalar(pair_bits[:], here[:].bitcast(I32), 2 ** PAIR_BITS - 1, None, ALU.bitwise_and))
            dve.tensor_copy(pair_f[:], pair_bits[:]).then_inc(pairs_known, 1)
            dve.wait_ge(edges_turned, 1)
            mark(dve.tensor_copy(row_before[:, 1:P + 1], p_hid[0][0:1, 0:P]))
            dve.tensor_copy(row_after[:, 0:P - 1], p_hid[0][0:1, P + 1:2 * P]).then_inc(edges_shifted, 1)
            link(dve.tensor_scalar(lower[:], code_here[:], float(SIGN_CODE), None, ALU.is_ge))
            dve.wait_ge(edges_back, 1)
            link(dve.tensor_copy(edge_words[:], p_hid[0][:, 2 * P:2 * P + 2]))
            link(dve.tensor_scalar(edge_codes[:], edge_words[:].bitcast(I32), PAIR_BITS, None, ALU.logical_shift_right))
            inside, head, tail = slice(1, COLS), slice(0, 1), slice(COLS - 1, COLS)
            before, after = slice(0, 1), slice(1, 2)
            mark(dve.tensor_tensor(same[:, inside], code_here[:, inside], code_here[:, 0:COLS - 1], ALU.is_equal))
            link(dve.tensor_tensor(same[:, head], code_here[:, head], edge_codes[:, before], ALU.is_equal))
            link(dve.tensor_scalar(floor_f[:], same[:], 2.0, -1.0, ALU.mult, ALU.add))
            dve.tensor_scalar(floor_f[:], floor_f[:], FLT_MAX, None, ALU.mult).then_inc(flags_ready, 1)
            link(dve.scalar_tensor_tensor(out=off[:], in0=lower[:], scalar=float(-SIGN_CODE), in1=code_here[:],
                                          op0=ALU.mult, op1=ALU.add))
            link(dve.tensor_scalar(back2[:], off[:], 2.0, 1.0 - 2 * CODE0, ALU.mult, ALU.add))
            link(dve.tensor_tensor(back2[:], back2[:], lower[:], ALU.mult))
            link(dve.scalar_tensor_tensor(out=node[:], in0=off[:], scalar=float(HALF - CODE0), in1=back2[:],
                                          op0=ALU.add, op1=ALU.subtract))
            ones = one[:, 0:1].broadcast_to([P, COLS])
            mark(dve.tensor_tensor_scan(count[:], same[:], ones, 0.0, ALU.mult, ALU.add))
            dve.tensor_reduce(whole[:], same[:], AX_X, ALU.min).then_inc(counts_local, 1)
            mark(dve.tensor_copy(ends[:, 0:COLS - 1], same[:, inside]))
            link(dve.tensor_tensor(ends[:, tail], code_here[:, tail], edge_codes[:, after], ALU.is_equal))
            dve.wait_ge(counts_turned, 1)
            mark(dve.tensor_copy(row_node[:], p_hid[1][0:1, 2 * P:3 * P]))
            link(dve.tensor_copy(row_ends[:], p_hid[1][0:1, 0:2 * P]))
            dve.tensor_tensor_scan(row_counts[:, 1:P + 1], row_ends[:, P:2 * P], row_ends[:, 0:P], 0.0,
                                   ALU.mult, ALU.add).then_inc(rows_counted, 1)
            link(dve.tensor_scalar(half_tile[:], row_node[:, GUARDED * PER:GUARDED * PER + 1], TILE_BITS + 1, None,
                                   ALU.logical_shift_right))
            dve.tensor_scalar(c0_need[:], half_tile[:], 1.0, float(C0_PAIRS), ALU.add, ALU.min).then_inc(c0_need_ready, 1)
            mark(dve.tensor_tensor(twin[:, inside], here[:, inside], here[:, 0:COLS - 1], ALU.is_equal))
            mark(dve.tensor_tensor(twin[:, head], here[:, head], edge_words[:, before], ALU.is_equal))
            link(dve.tensor_scalar(skip[:], ends[:], SKIP, 1.0, ALU.mult, ALU.add))
            dve.scalar_tensor_tensor(out=row_f[:], in0=node[:], scalar=2.0, in1=skip[:],
                                     op0=ALU.mult, op1=ALU.add).then_inc(tables, 1)
            dve.wait_ge(carry_turned, 1)
            link(dve.tensor_copy(carry[:], p_hid[1][:, 3 * P:3 * P + 1]))
            link(dve.tensor_tensor_scan(count[:], same[:], ones, carry[:, 0:1], ALU.mult, ALU.add))
            dve.reciprocal(inverse[:], count[:]).then_inc(inverse_ready, 1)

            def l0_pick(s, n):
                g = s * PER + n
                at = group_of(s, n)
                dve.wait_ge(gathered[n], (s + 1) * 16 * TILES)
                dve.tensor_tensor(wrong[n][:], pairs[n][:, :, SRC], node_at[:, at, :].rearrange("p a t -> p (a t)"),
                                  ALU.not_equal).then_inc(edge_known, 1)
                dve.wait_ge(edge_known, g + 1)
                dve.tensor_tensor(odd[n][:], wrong[n][:], twin_at[:, at, :].rearrange("p a t -> p (a t)"),
                                  ALU.max).then_inc(edge_odd, 1)
                dve.wait_ge(edge_odd, g + 1)
                dve.sem_inc(dve_stands, 1)
                dve.copy_predicated(out=pairs[n][:, :, 0:EFEAT], mask=odd[n][:].unsqueeze(2).broadcast_to([P, TILES, EFEAT]),
                                    data=pairs[n][:, :, EFEAT:2 * EFEAT]).then_inc(edge_picked, 1)
                dve.copy_predicated(out=pairs[n][:, :, DST], mask=odd[n][:],
                                    data=pairs[n][:, :, DST + 2]).then_inc(dst_picked, 1)
                dve.wait_ge(dst_picked, g + 1)
                dve.tensor_copy(dst_idx[:, at, :].rearrange("p a t -> p (a t)"), pairs[n][:, :, DST]).then_inc(dst_kept, 1)

            def l0_scan(s, n, first=False):
                g = s * PER + n
                dve.wait_ge(attrs_turned, g + 1)
                dve.wait_ge(flags_in[n], (s + 1) * 32)
                if not first:
                    dve.wait_ge(hid_psum, (s - 1) * PER + n + 1)
                if not (first and n == 0):
                    dve.wait_ge(maxed, g)
                dve.tensor_tensor_scan(feats[n][0:EFEAT, :], same_b[n][0:EFEAT, :], p_feat[n][0:EFEAT, :],
                                       feats[1 - n][0:EFEAT, COLS - 1:COLS], ALU.mult, ALU.add).then_inc(summed, 1)
                dve.tensor_tensor_scan(feats[n][EFEAT:2 * EFEAT, :], floor_b[n][:], p_feat[n][0:EFEAT, :],
                                       feats[1 - n][EFEAT:2 * EFEAT, COLS - 1:COLS], ALU.min, ALU.max).then_inc(maxed, 1)
                dve.wait_ge(summed, g + 1)
                dve.wait_ge(inverse_in[n], (s + 1) * 16)
                dve.tensor_tensor(feats[n][2 * EFEAT:3 * EFEAT, :], feats[n][0:EFEAT, :], inverse_b[n][:],
                                  ALU.mult).then_inc(averaged, 1)

            def l0_delta(s, n, first=False):
                dve.wait_ge(delta_psum, s * PER + n + 1)
                if not first:
                    dve.wait_ge(scattered[n], s * 16 * TILES)
                dve.tensor_tensor(delta[n][:], p_rows[:, n, :, :],
                                  b2_b[:].unsqueeze(1).broadcast_to([P, TILES, FEAT]), ALU.add).then_inc(delta_ready, 1)

            def l0_centre(s, first=False):
                dve.wait_ge(x_in, (s + 1) * 16)
                dve.tensor_reduce(xsum[:], x_tile, AX_X, ALU.add).then_inc(xsum_ready, 1)
                dve.wait_ge(xsum_ready, s + 1)
                dve.tensor_scalar(xmean[:], xsum[:], 1.0 / FEAT, None, ALU.mult).then_inc(xmean_ready, 1)
                dve.wait_ge(xmean_ready, s + 1)
                if not first:
                    dve.wait_ge(x_out, s * 16)
                dve.tensor_tensor(xc, x_tile, xmean[:].unsqueeze(2).broadcast_to([P, TROWS, FEAT]),
                                  ALU.subtract).then_inc(xc_ready, 1)

            def l0_dve(s, first=False):
                for n in range(PER):
                    l0_pick(s, n)
                    l0_scan(s, n, first)
                l0_centre(s, first)
                for n in range(PER):
                    l0_delta(s, n, first)

            dve.wait_ge(idx_kept, 3)
            l0_dve(0, first=True)

            mark(dve.memset(settled[:], 0.0))
            mark(dve.memset(normed[:, 0:1], 0.0))
            link(dve.tensor_scalar(row_tile[:], row_node[:], TILE_BITS, None, ALU.logical_shift_right))
            first_rows = slice(PER, PER * (STEPS - SETTLE), PER)
            link(dve.tensor_copy(settled[:, SETTLE + 1:STEPS], row_tile[:, first_rows]))
            link(dve.tensor_tensor_scan(normed[:, 1:STEPS + 1], one[0:1, 0:1].broadcast_to([1, STEPS]), settled[:],
                                        0.0, ALU.add, ALU.min))
            link(dve.tensor_tensor(idle[:], normed[:, 0:STEPS], normed[:, 1:STEPS + 1], ALU.is_equal))
            mark(dve.scalar_tensor_tensor(out=plan[:, 0:STEPS], in0=idle[:], scalar=float(NO_TILE), in1=normed[:, 0:STEPS],
                                          op0=ALU.mult, op1=ALU.add))
            dve.tensor_copy(plan[:, STEPS:STEPS + 1], normed[:, STEPS:STEPS + 1]).then_inc(plan_ready, 1)

            with dve.Fori(1, STEPS) as s:
                l0_dve(s)

            dve.tensor_scalar(g_idx[:], row_idx[:], -1.0, 0.5, ALU.add, ALU.mult).then_inc(g_idx_ready, 1)

            inv = 1.0 / FEAT

            def rows_b(a, rows):
                return a[:, rows].unsqueeze(2).broadcast_to([P, rows.stop - rows.start, FEAT])

            def l1_add(s, first=False):
                if not first:
                    dve.wait_ge(x1_ready, s * 2)
                dve.wait_ge(l1_gathered, (s + 1) * 16 * STEP_CHUNKS)
                dve.wait_ge(tile_in, (s + 1) * 16)
                dve.tensor_tensor(y, near[:, :, 0, :], near[:, :, 1, :], ALU.add).then_inc(y_ready, 1)

            def l1_variance(s):
                dve.wait_ge(ysq_ready, s + 1)
                dve.tensor_reduce(yvar[:], ysq, AX_X, ALU.add).then_inc(yvar_ready, 1)

            def l1_scale(s, first=False):
                dve.wait_ge(ystd_ready, s + 1)
                dve.reciprocal(yrstd[:], ystd[:]).then_inc(yrstd_ready, 1)
                dve.wait_ge(yrstd_ready, s + 1)
                if not first:
                    dve.wait_ge(x1_turned, s * PER)
                    dve.wait_ge(x1_out, s * 16)
                for rows in (slice(0, STEP_CHUNKS), slice(STEP_CHUNKS, LN_ROWS)):
                    dve.tensor_tensor(x1[:, rows, :], y[:, rows, :], rows_b(yrstd, rows), ALU.mult).then_inc(x1_ready, 1)

            def l1_sum(s, first=False):
                for n in range(PER):
                    g = s * PER + n
                    dve.wait_ge(x1_turned, g + 1)
                    dve.wait_ge(l1_flags_in[n], (s + 1) * 16)
                    if not first:
                        dve.wait_ge(g_psum, (s - 1) * PER + n + 1)
                    if not (first and n == 0):
                        dve.wait_ge(aggr_ready, g)
                    dve.tensor_tensor_scan(aggr[n][:], same_b[n][:], p_feat[n][:], aggr[1 - n][:, COLS - 1:COLS],
                                           ALU.mult, ALU.add).then_inc(aggr_ready, 1)

            def l1_bias(s):
                dve.wait_ge(g_psum, (s + 1) * PER)
                dve.tensor_tensor(gz[:].rearrange("p (n t) f -> p n t f", n=PER), p_rows,
                                  b_b[:].unsqueeze(1).unsqueeze(1).broadcast_to([P, PER, TILES, FEAT]),
                                  ALU.add).then_inc(gz_ready, 1)

            def l1_mean(s):
                dve.wait_ge(gr_ready, s + 1)
                dve.tensor_reduce(gsum[:], gr[:], AX_X, ALU.add).then_inc(gsum_ready, 1)
                dve.wait_ge(gsum_ready, s + 1)
                dve.tensor_scalar(gmean[:], gsum[:], inv, None, ALU.mult).then_inc(gmean_ready, 1)

            def l1_centre(s, first=False):
                dve.wait_ge(gmean_ready, s + 1)
                if not first:
                    dve.wait_ge(l1_scattered, s * 16 * STEP_CHUNKS)
                for n in range(PER):
                    rows = slice(n * TILES, (n + 1) * TILES)
                    ins = dve.tensor_tensor(delta[n][:], gr[:, rows, :], rows_b(gmean, rows), ALU.subtract)
                ins.then_inc(g_ready, 1)

            def norm_add(t):
                dve.wait_ge(z_done, t + 1)
                dve.sem_inc(dve_stands, 1)
                dve.wait_ge(z_in, (t + 1) * 32)
                dve.tensor_tensor(z, in_x1, in_g, ALU.add).then_inc(z_added, 1)

            def norm_variance(t):
                dve.wait_ge(z_squared, t + 1)
                dve.tensor_reduce(zvar[:], zsq, AX_X, ALU.add).then_inc(zvar_ready, 1)

            def norm_scale(t):
                dve.wait_ge(zstd_ready, t + 1)
                dve.reciprocal(zrstd[:], zstd[:]).then_inc(zrstd_ready, 1)
                dve.wait_ge(zrstd_ready, t + 1)
                dve.sem_inc(dve_stands, 1)
                dve.wait_ge(out_done, (t + 1) * 16)
                dve.tensor_tensor(z_out, z, rows_b(zrstd, slice(0, TROWS)), ALU.mult).then_inc(z_done, 1)

            def l1_rest(s, tile=None, first=False):
                if tile is not None:
                    norm_add(tile)
                l1_bias(s - 1)
                l1_variance(s)
                if tile is not None:
                    norm_variance(tile)
                l1_scale(s)
                l1_mean(s - 1)
                l1_sum(s)
                l1_centre(s - 1, first)
                if tile is not None:
                    norm_scale(tile)

            for n in range(PER):
                dve.wait_ge(scattered[n], 16 * TILES * STEPS)
            dve.wait_ge(x_out, 16 * STEPS)
            dve.sem_inc(z_added, 1)
            dve.sem_inc(z_done, 1)
            l1_add(0, first=True)
            l1_variance(0)
            l1_scale(0, first=True)
            l1_sum(0, first=True)
            l1_add(1)
            l1_rest(1, first=True)
            with dve.Fori(2, STEPS) as s:
                tile = dve.value_load(plan[0:1, bass.ds(s, 1)], min_val=0, max_val=NO_TILE + STEPS)
                l1_add(s)
                with dve.If(tile < NO_TILE):
                    l1_rest(s, planned(tile))
                with dve.Else():
                    l1_rest(s)
            l1_bias(STEPS - 1)
            l1_mean(STEPS - 1)
            l1_centre(STEPS - 1)

            done = dve.value_load(plan[0:1, STEPS:STEPS + 1], min_val=0, max_val=STEPS - SETTLE - 1)
            with dve.Fori(done, STEPS - 1) as t:
                norm_add(t)
                norm_variance(t)
                norm_scale(t)
            norm_add(STEPS - 1)
            norm_variance(STEPS - 1)
            norm_scale(STEPS - 1)


_INS = ["x", "src", "dst", "edge_attr_32", "L0_gnn_u", "L0_gnn_W1", "L0_gnn_b1", "L0_gnn_W2", "L0_gnn_b2", "L1_gnn_W", "L1_gnn_b"]


def kernel(**inputs):
    import numpy as _np
    import concourse.bacc as _bacc
    from concourse import mybir as _mybir
    from concourse.bass_utils import run_bass_kernel_spmd as _run

    nc = _bacc.Bacc("TRN2", target_bir_lowering=False, num_devices=1)
    arrays, args = {}, []
    for name in _INS:
        a = _np.ascontiguousarray(inputs[name])
        arrays[f"in_{name}"] = a
        args.append(nc.dram_tensor(f"in_{name}", a.shape, _mybir.dt.from_np(a.dtype), kind="ExternalInput").ap())
    args.append(nc.dram_tensor("out_0", (NODES, FEAT), F32, kind="ExternalOutput").ap())
    gnn_kernel(nc, *args)
    r = _run(nc, [arrays], core_ids=[0])
    return r.results[0]["out_0"]
```
